# Optimizing a Trainium2 kernel written in Bass

```python
import numpy as np
import jax
import jax.numpy as jnp

def _softmax(x, axis=-1):
    return jax.nn.softmax(x, axis=axis)

def _gelu(x):
    return jax.nn.gelu(x, approximate=True)

def _silu(x):
    return jax.nn.silu(x)

def _sigmoid(x):
    return jax.nn.sigmoid(x)

def _layernorm(x, axis=-1, eps=1e-05):
    m = jnp.mean(x, axis=axis, keepdims=True)
    v = jnp.var(x, axis=axis, keepdims=True)
    return (x - m) / jnp.sqrt(v + eps)

def _scatter_add(tgt, idx, src, axis=0):
    return tgt.at[idx].add(src)

def _segment_sum(src, seg, n):
    return jax.ops.segment_sum(src, seg, n)
kernel_name = 'mk_prb_d1_jaxref_r4_402321'

def setup_inputs(seed: int=0):
    np.random.seed(seed)
    _w = jnp.asarray

    def _L0_attn_setup():
        import jax, jax.numpy as jnp
        import numpy as np
        _A = np.array([[1, 1, 1, 0, 1, 1, 1, 0, 0, 0, 1, 1], [1, 1, 0, 1, 1, 1, 0, 0, 0, 1, 1, 0], [1, 0, 1, 1, 1, 0, 0, 0, 1, 1, 0, 1], [0, 1, 1, 1, 0, 0, 0, 1, 1, 0, 1, 1], [0, 0, 0, 0, 1, 1, 1, 1, 1, 1, 1, 1], [1, 1, 1, 1, 0, 0, 0, 0, 0, 0, 0, 0], [0, 0, 0, 0, 1, 1, 1, 1, 0, 0, 0, 0], [1, 1, 0, 0, 1, 1, 0, 0, 1, 1, 0, 0], [1, 0, 1, 0, 1, 0, 1, 0, 1, 0, 1, 0], [0, 1, 0, 1, 0, 1, 0, 1, 0, 1, 0, 1], [1, 0, 0, 1, 1, 0, 0, 1, 1, 0, 0, 1], [0, 1, 1, 0, 0, 1, 1, 0, 0, 1, 1, 0]], dtype=np.float32)
        _H = jnp.asarray(np.concatenate([_A.T, np.eye(12, dtype=np.float32)], axis=1))

        def _fractal_dimension(x):
            s = x.reshape(-1)
            sn = (s - s.min()) / (s.max() - s.min() + 1e-10)
            counts = []
            for sc in (2, 4, 8, 16, 32):
                blk = sn[:sc * sc]
                counts.append(jnp.maximum(jnp.sum(blk > blk.mean()).astype(jnp.float32), 1.0))
            lx = jnp.log(jnp.array([2.0, 4.0, 8.0, 16.0, 32.0], dtype=jnp.float32))
            ly = jnp.log(jnp.stack(counts))
            n = jnp.float32(5.0)
            num = n * jnp.sum(lx * ly) - jnp.sum(lx) * jnp.sum(ly)
            den = n * jnp.sum(lx * lx) - jnp.sum(lx) ** 2
            return jnp.clip(-num / den, 1.0, 2.0)

        def _wave_filter(D, d):
            k = jnp.fft.fftfreq(d).astype(jnp.float32)
            ka = jnp.abs(k) + 1e-08
            omega = 1.0 + 0.2 * D
            a = 1.0 + 0.5 * D
            b = 0.1 * D
            real = jnp.sin(omega * D + a * ka)
            phase = omega * D - ka + b * ka ** 2
            return real * jnp.exp(1j * phase)

        def _golay_correct(bits):
            syn = (bits @ _H.T > 0.5).astype(jnp.float32)
            w = syn.sum(-1)
            _, idx = jax.lax.top_k(syn, 3)
            take = (jnp.arange(3)[None, :] < jnp.minimum(w, 3.0)[:, None]).astype(jnp.float32)
            pattern = (jax.nn.one_hot(idx, 24, dtype=jnp.float32) * take[..., None]).sum(axis=1)
            do_fix = ((w > 0) & (w <= 3))[:, None]
            return jnp.where(do_fix, jnp.mod(bits + pattern, 2.0), bits)
        key = jax.random.key(seed)
        k1, k2, k3 = jax.random.split(key, 3)
        B, S, E = (8, 512, 256)
        x = jax.random.normal(k1, (B, S, E), dtype=jnp.float32)
        W_el = jax.random.normal(k2, (E, 24), dtype=jnp.float32) * 0.02
        b_el = jnp.zeros((24,), dtype=jnp.float32)
        W_le = jax.random.normal(k3, (24, E), dtype=jnp.float32) * 0.02
        b_le = jnp.zeros((E,), dtype=jnp.float32)
        return {'x': x, 'W_el': W_el, 'b_el': b_el, 'W_le': W_le, 'b_le': b_le}
    _L0_attn_in = _L0_attn_setup()

    def _L0_ffn_setup():
        import jax, jax.numpy as jnp
        import numpy as np
        N_EMBD = 256
        N_STATE = 1024
        key = jax.random.key(seed)
        k_x, k_w1, k_b1, k_w2, k_b2 = jax.random.split(key, 5)
        x = jax.random.normal(k_x, (4, 512, N_EMBD), dtype=jnp.float32)
        w1 = jax.random.normal(k_w1, (N_EMBD, N_STATE), dtype=jnp.float32) * (1.0 / np.sqrt(N_EMBD))
        b1 = jax.random.normal(k_b1, (N_STATE,), dtype=jnp.float32) * 0.02
        w2 = jax.random.normal(k_w2, (N_STATE, N_EMBD), dtype=jnp.float32) * (1.0 / np.sqrt(N_STATE))
        b2 = jax.random.normal(k_b2, (N_EMBD,), dtype=jnp.float32) * 0.02
        return {'x': x, 'w1': w1, 'b1': b1, 'w2': w2, 'b2': b2}
    _L0_ffn_in = _L0_ffn_setup()
    _d = {'L0_attn_x': _L0_attn_in['x'], 'L0_attn_W_el': _L0_attn_in['W_el'], 'L0_attn_b_el': _L0_attn_in['b_el'], 'L0_attn_W_le': _L0_attn_in['W_le'], 'L0_attn_b_le': _L0_attn_in['b_le'], 'L0_ffn_w1': _L0_ffn_in['w1'], 'L0_ffn_b1': _L0_ffn_in['b1'], 'L0_ffn_w2': _L0_ffn_in['w2'], 'L0_ffn_b2': _L0_ffn_in['b2']}
    _x0 = _d['L0_attn_x']
    _d['L0_attn_x'] = jax.random.normal(jax.random.fold_in(jax.random.key(seed), 1), (2, 4096, 256), dtype=_x0.dtype)
    del _x0
    return _d

def reference(L0_attn_x, L0_attn_W_el, L0_attn_b_el, L0_attn_W_le, L0_attn_b_le, L0_ffn_w1, L0_ffn_b1, L0_ffn_w2, L0_ffn_b2):

    def _L0_attn_ref(x, W_el, b_el, W_le, b_le):
        import jax, jax.numpy as jnp
        import numpy as np
        _A = np.array([[1, 1, 1, 0, 1, 1, 1, 0, 0, 0, 1, 1], [1, 1, 0, 1, 1, 1, 0, 0, 0, 1, 1, 0], [1, 0, 1, 1, 1, 0, 0, 0, 1, 1, 0, 1], [0, 1, 1, 1, 0, 0, 0, 1, 1, 0, 1, 1], [0, 0, 0, 0, 1, 1, 1, 1, 1, 1, 1, 1], [1, 1, 1, 1, 0, 0, 0, 0, 0, 0, 0, 0], [0, 0, 0, 0, 1, 1, 1, 1, 0, 0, 0, 0], [1, 1, 0, 0, 1, 1, 0, 0, 1, 1, 0, 0], [1, 0, 1, 0, 1, 0, 1, 0, 1, 0, 1, 0], [0, 1, 0, 1, 0, 1, 0, 1, 0, 1, 0, 1], [1, 0, 0, 1, 1, 0, 0, 1, 1, 0, 0, 1], [0, 1, 1, 0, 0, 1, 1, 0, 0, 1, 1, 0]], dtype=np.float32)
        _H = jnp.asarray(np.concatenate([_A.T, np.eye(12, dtype=np.float32)], axis=1))

        def _fractal_dimension(x):
            s = x.reshape(-1)
            sn = (s - s.min()) / (s.max() - s.min() + 1e-10)
            counts = []
            for sc in (2, 4, 8, 16, 32):
                blk = sn[:sc * sc]
                counts.append(jnp.maximum(jnp.sum(blk > blk.mean()).astype(jnp.float32), 1.0))
            lx = jnp.log(jnp.array([2.0, 4.0, 8.0, 16.0, 32.0], dtype=jnp.float32))
            ly = jnp.log(jnp.stack(counts))
            n = jnp.float32(5.0)
            num = n * jnp.sum(lx * ly) - jnp.sum(lx) * jnp.sum(ly)
            den = n * jnp.sum(lx * lx) - jnp.sum(lx) ** 2
            return jnp.clip(-num / den, 1.0, 2.0)

        def _wave_filter(D, d):
            k = jnp.fft.fftfreq(d).astype(jnp.float32)
            ka = jnp.abs(k) + 1e-08
            omega = 1.0 + 0.2 * D
            a = 1.0 + 0.5 * D
            b = 0.1 * D
            real = jnp.sin(omega * D + a * ka)
            phase = omega * D - ka + b * ka ** 2
            return real * jnp.exp(1j * phase)

        def _golay_correct(bits):
            syn = (bits @ _H.T > 0.5).astype(jnp.float32)
            w = syn.sum(-1)
            _, idx = jax.lax.top_k(syn, 3)
            take = (jnp.arange(3)[None, :] < jnp.minimum(w, 3.0)[:, None]).astype(jnp.float32)
            pattern = (jax.nn.one_hot(idx, 24, dtype=jnp.float32) * take[..., None]).sum(axis=1)
            do_fix = ((w > 0) & (w <= 3))[:, None]
            return jnp.where(do_fix, jnp.mod(bits + pattern, 2.0), bits)
        B, S, E = x.shape
        D = _fractal_dimension(x)
        filt = _wave_filter(D, E)
        x1 = jnp.fft.ifft(jnp.fft.fft(x, axis=-1) * filt, axis=-1).real.astype(x.dtype)
        lat = x1 @ W_el + b_el
        bits = (jax.nn.sigmoid(lat) > 0.5).astype(jnp.float32).reshape(B * S, 24)
        corrected = _golay_correct(bits).reshape(B, S, 24)
        return x1 + corrected @ W_le + b_le

    def _L0_ffn_ref(x, w1, b1, w2, b2):
        import jax, jax.numpy as jnp
        import numpy as np
        N_EMBD = 256
        N_STATE = 1024
        h = jax.nn.gelu(jnp.einsum('bse,eh->bsh', x, w1) + b1, approximate=False)
        return jnp.einsum('bsh,he->bse', h, w2) + b2
    x = L0_attn_x
    xn = _layernorm(x, axis=-1)
    x = x + _L0_attn_ref(xn, L0_attn_W_el, L0_attn_b_el, L0_attn_W_le, L0_attn_b_le) + _L0_ffn_ref(xn, L0_ffn_w1, L0_ffn_b1, L0_ffn_w2, L0_ffn_b2)
    return x

_drawn_inputs = setup_inputs


def setup_inputs(seed=0):
    import zlib

    import numpy as np

    out = dict(_drawn_inputs(seed))
    spreads = {'L0_attn_b_el': (0.0, 0.371), 'L0_attn_b_le': (0.0, 0.1)}
    factors = {'L0_ffn_b1': 7.17, 'L0_ffn_b2': 4.921}
    for name, (base, spread) in spreads.items():
        noise = np.random.default_rng([zlib.crc32(name.encode()), seed]).standard_normal(out[name].shape)
        drawn = base * np.exp(spread * noise) if base else spread * noise
        out[name] = jnp.asarray(drawn.astype(out[name].dtype))
    for name, factor in factors.items():
        out[name] = (out[name] * factor).astype(out[name].dtype)
    return out
```

```python
import math
from contextlib import ExitStack

import concourse.bass as bass
from concourse import mybir

F32, F32R, BF16, I32 = mybir.dt.float32, mybir.dt.float32r, mybir.dt.bfloat16, mybir.dt.int32
ALU = mybir.AluOpType
ACT = mybir.ActivationFunctionType
AX = mybir.AxisListType

P = 128
TOKENS, E, HID, LAT, SYN = 2 * 4096, 256, 1024, 24, 12
TILES = TOKENS // P
CT = 4
CTOK = CT * P
CHUNKS = TILES // CT
KB = E // P
MB = HID // P
PAIRS = CT // 2
CE = E + LAT
HR = 4
BANK = 512
SCALES = (2, 4, 8, 16, 32)
PREFIX = [s * s for s in SCALES]
FR = max(PREFIX) // E
LN_EPS = 1e-5
SEG = 32
PRIMED = 1
ROWS_LE = LAT + 2

K_ID = 0
K_INVN = K_ID + P
K_COEF = K_INVN + 5
K_KA = K_COEF + 5
K_KA2 = K_KA + KB
K_WK = K_KA2 + KB
K_POW2 = K_WK + KB
K_END = K_POW2 + LAT


def build(nc, x, w_el, b_el, w_le, b_le, w1, b1, w2, b2, consts, basis, masks, out):
    ctx = ExitStack()
    with ctx:
        def sb(name, shape, dt):
            return ctx.enter_context(nc.sbuf_tensor(name, shape, dt))

        def ps(name, shape, dt):
            return ctx.enter_context(nc.psum_tensor(name, shape, dt))

        def sem(name):
            return ctx.enter_context(nc.semaphore(name))

        x_sb = sb("x_sb", [P, TILES * E], F32)
        xn = sb("xn", [P, CT, E], F32)
        xT_hi = [sb(f"xT_hi{i}", [P, KB, CTOK], F32R) for i in range(2)]
        xT_lo = [sb(f"xT_lo{i}", [P, KB, CTOK], F32R) for i in range(2)]
        h = [sb(f"h{i}", [P, CTOK], F32) for i in range(2)]
        h_hi = [sb(f"h_hi{i}", [P, CTOK], F32R) for i in range(HR)]
        h_lo = [sb(f"h_lo{i}", [P, CTOK], F32R) for i in range(HR)]
        w1_f = sb("w1_f", [P, KB, HID], F32)
        w1_hi = sb("w1_hi", [P, KB, MB, P], F32R)
        w1_lo = sb("w1_lo", [P, KB, MB, P], F32R)
        w2_f = sb("w2_f", [P, MB, E], F32)
        w2_hi = sb("w2_hi", [P, MB, E], F32R)
        w2_lo = sb("w2_lo", [P, MB, E], F32R)
        b1_sb = sb("b1_sb", [P, MB], F32)
        con = sb("con", [P, K_END], F32)
        mask_sb = sb("mask_sb", [P, SYN], I32)
        bel_sb = sb("bel_sb", [P, LAT], F32)
        wel_sb = sb("wel_sb", [P, KB, LAT], F32)
        basis_sb = sb("basis_sb", [P, KB, E], F32)
        basis_w = sb("basis_w", [P, KB, E], F32)
        c_f = sb("c_f", [P, KB, E], F32)
        c_hi = sb("c_hi", [P, KB, CE], F32R)
        c_lo = sb("c_lo", [P, KB, CE], F32R)
        stats = sb("stats", [P, CT, 6], F32)
        mv = [sb(f"mv{i}", [P, CT, 2], F32) for i in range(2)]
        var_eps = sb("var_eps", [P, CT], F32)
        rstd = [sb(f"rstd{i}", [P, CT], F32) for i in range(2)]
        eps = sb("eps", [P, CT], F32)
        minus_half = sb("minus_half", [P, CT], F32)
        fr_x = sb("fr_x", [P, FR, E], F32)
        fr_gt = sb("fr_gt", [P, FR * E], BF16)
        fr_stats = sb("fr_stats", [P, FR, 6], F32)
        fr_mv = sb("fr_mv", [P, FR, 2], F32)
        fr_ve = sb("fr_ve", [P, FR], F32)
        fr_rstd = sb("fr_rstd", [P, FR], F32)
        fr_sum = sb("fr_sum", [P, 5], F32)
        fr_mean = sb("fr_mean", [P, 5], F32)
        fr_cnt = sb("fr_cnt", [P, 5], F32)
        fr_cnt1 = sb("fr_cnt1", [P, 5], F32)
        fr_ln = sb("fr_ln", [P, 5], F32)
        fr_ly = sb("fr_ly", [P, 5], F32)
        fr_d = sb("fr_d", [P, 8], F32)
        wave = sb("wave", [P, 4, 2 * KB], F32)
        filt = sb("filt", [P, 2, KB], F32)
        bits = sb("bits", [P, 2, LAT], F32)
        weighed = sb("weighed", [P, 2, LAT], F32)
        word = sb("word", [P, 2, 1], I32)
        met = sb("met", [P, 2, SYN], I32)
        syn = sb("syn", [P, 2, SYN], F32)
        weight = sb("weight", [P, 2, 1], F32)
        flips = sb("flips", [P, 2, SYN], F32)
        cor = sb("cor", [P, 2, 3, SEG], BF16)
        cor_T = sb("cor_T", [3 * SEG, 2 * P], BF16)
        id_bf = sb("id_bf", [P, P], BF16)
        le_f = sb("le_f", [ROWS_LE, E], F32)
        le_r1 = sb("le_r1", [ROWS_LE, E], F32)
        le_mid = sb("le_mid", [ROWS_LE, E], BF16)
        le3 = sb("le3", [3 * SEG, E], BF16)

        p_h = ps("p_h", [P, 2, BANK], F32)
        p_o = ps("p_o", [P, CT, E], F32)
        p_c = ps("p_c", [P, 2, BANK], F32)
        p_t = ps("p_t", [P, BANK], F32)
        p_g = ps("p_g", [P, 2 * BANK], BF16)

        x_in = [sem("x_even"), sem("x_odd")]
        w1_in, w2_in, b1_in, con_in, fr_in = sem("w1_in"), sem("w2_in"), sem("b1_in"), sem("con_in"), sem("fr_in")
        basis_in, small_in, le_in = sem("basis_in"), sem("small_in"), sem("le_in")
        stored = sem("stored")
        pool_set = sem("pool_set")
        id_ready = sem("id_ready")
        w1_hi_ready, w1_ready = sem("w1_hi_ready"), sem("w1_ready")
        w2_hi_ready, w2_ready = sem("w2_hi_ready"), sem("w2_ready")
        fr_stat, fr_veps, fr_rs = sem("fr_stat"), sem("fr_veps"), sem("fr_rs")
        counted, logged, argued, sined = sem("counted"), sem("logged"), sem("argued"), sem("sined")
        basis_wd, c_made, c_copied = sem("basis_wd"), sem("c_made"), sem("c_copied")
        cw_made, cw_hi, c_ready = sem("cw_made"), sem("cw_hi"), sem("c_ready")
        le_ready = sem("le_ready")
        stat_done = sem("stat_done")
        veps_done, rstd_done = sem("veps_done"), sem("rstd_done")
        xn_done = sem("xn_done")
        t_done = sem("t_done")
        t_hi, t_lo = sem("t_hi"), sem("t_lo")
        up_done = sem("up_done")
        gelu_done, h_hi_done, h_lo_done = sem("gelu_done"), sem("h_hi_done"), sem("h_lo_done")
        down_done = sem("down_done")
        ffn_out = sem("ffn_out")
        wave_done = sem("wave_done")
        cor_done, cor_t, cor_sb = sem("cor_done"), sem("cor_t"), sem("cor_sb")
        le_done = sem("le_done")
        pair_out = sem("pair_out")
        link = sem("link")

        x_rows = x.rearrange("b s e -> (b s) e").rearrange("(p t) e -> p (t e)", p=P)
        out_rows = out.rearrange("b s e -> (b s) e").rearrange("(p t) e -> p (t e)", p=P)
        CW = CT * E
        block = ctx.enter_context(nc.Block())

        @block.sync
        def _(sp):
            sp.dma_start(x_sb[:, 0:CW], x_rows[:, 0:CW]).then_inc(x_in[0], 16)
            sp.dma_start(w1_f[:, 0, :], w1[0:P, :]).then_inc(w1_in, 16)
            sp.dma_start(w1_f[:, 1, :], w1[P:2 * P, :]).then_inc(w1_in, 16)
            sp.dma_start(x_sb[:, CW:2 * CW], x_rows[:, CW:2 * CW]).then_inc(x_in[1], 16)
            with sp.Fori(1, CHUNKS // 2) as i:
                for par in range(2):
                    sp.wait_ge(x_in[par], i * 16)
                    at = i * (2 * CW) + par * CW
                    sp.dma_start(x_sb[:, bass.ds(at, CW)], x_rows[:, bass.ds(at, CW)]).then_inc(x_in[par], 16)
            with sp.Fori(0, CHUNKS * PAIRS) as n:
                sp.wait_ge(pair_out, PRIMED + n + 1)
                sp.dma_start(out_rows[:, bass.ds(n * (2 * E), 2 * E)],
                             x_sb[:, bass.ds(n * (2 * E), 2 * E)]).then_inc(stored, 16)
            sp.wait_ge(stored, 16 * CHUNKS * PAIRS)

        @block.gpsimd
        def _(pool):
            nc.gpsimd.memset(eps[:], LN_EPS).then_inc(pool_set, 1)
            nc.gpsimd.memset(minus_half[:], -0.5).then_inc(pool_set, 1)
            pool.wait_ge(pool_set, 2)

            def inverse_root(c, par):
                pool.wait_ge(stat_done, c + 1)
                nc.gpsimd.tensor_tensor(var_eps[:], mv[par][:, :, 1], eps[:], ALU.add).then_inc(veps_done, 1)
                pool.wait_ge(veps_done, c + 1)
                nc.gpsimd.tensor_tensor(rstd[par][:], var_eps[:], minus_half[:], ALU.pow).then_inc(rstd_done, 1)

            inverse_root(0, 0)
            pool.wait_ge(fr_stat, 1)
            nc.gpsimd.tensor_tensor(fr_ve[:], fr_mv[:, :, 1], eps[:], ALU.add).then_inc(fr_veps, 1)
            pool.wait_ge(fr_veps, 1)
            nc.gpsimd.tensor_tensor(fr_rstd[:], fr_ve[:], minus_half[:], ALU.pow).then_inc(fr_rs, 1)
            inverse_root(1, 1)
            with pool.Fori(0, (CHUNKS - 2) // 2) as i:
                for u in range(2):
                    inverse_root(2 * i + 2 + u, u)

        @block.scalar
        def _(act):
            act.dma_start(con[:], consts).then_inc(con_in, 16)
            act.dma_start(fr_x[:, :, :].rearrange("p a e -> p (a e)"),
                          x[0, 0:FR, :].rearrange("a e -> (a e)").partition_broadcast(P)).then_inc(fr_in, 16)
            act.dma_start(b1_sb[:], b1.rearrange("(p m) -> p m", m=MB)).then_inc(b1_in, 16)
            act.dma_start(w2_f[:, :, :], w2.rearrange("(p m) e -> p m e", m=MB)).then_inc(w2_in, 16)
            act.dma_start(basis_sb[:, :, :], basis.rearrange("(k p) e -> p k e", p=P)).then_inc(basis_in, 16)
            act.dma_start(wel_sb[:, :, :], w_el.rearrange("(k p) l -> p k l", p=P)).then_inc(small_in, 16)
            act.dma_start(mask_sb[:], masks).then_inc(small_in, 16)
            act.dma_start(bel_sb[:], b_el.partition_broadcast(P)).then_inc(small_in, 16)
            act.dma_start(le_f[0:LAT, :], w_le).then_inc(le_in, 16)
            act.dma_start(le_f[LAT:LAT + 1, :], b_le[None, :]).then_inc(le_in, 16)
            act.dma_start(le_f[LAT + 1:LAT + 2, :], b2[None, :]).then_inc(le_in, 16)

            act.sem_inc(cor_sb, PRIMED)

            def transposed_hi(c, par, k):
                act.wait_ge(t_done, KB * c + k + 1)
                nc.scalar.copy(xT_hi[par][:, k, :], p_t[:]).then_inc(t_hi, 1)

            def gelu(c, m, first=False):
                act.wait_ge(up_done, MB * c + m + 1)
                if not (first and m < 2):
                    act.wait_ge(h_lo_done, MB * c + m - 1)
                nc.scalar.activation(h[m % 2][:], p_h[:, m % 2, :], ACT.Gelu,
                                     bias=b1_sb[:, m:m + 1]).then_inc(gelu_done, 1)

            def hidden_hi(c, m, first=False):
                act.wait_ge(gelu_done, MB * c + m + 1)
                if not (first and m < HR):
                    act.wait_ge(down_done, MB * c + m + 1 - HR)
                nc.scalar.copy(h_hi[m % HR][:], h[m % 2][:]).then_inc(h_hi_done, 1)

            def corrected_copy(c, q):
                act.wait_ge(cor_t, PRIMED + PAIRS * c + q + 1)
                act.wait_ge(le_done, PRIMED + PAIRS * c + q)
                nc.scalar.copy(cor_T[:], p_g[0:3 * SEG, 0:2 * P]).then_inc(cor_sb, 1)

            def chunk(c, par, wave=True, following=True):
                for m in range(MB):
                    gelu(c, m)
                    if m == MB - 1 and following:
                        transposed_hi(c + 1, 1 - par, 1)
                    hidden_hi(c, m)
                    if m == 2:
                        corrected_copy(c - 1, 0)
                    if m == 6:
                        corrected_copy(c - 1, 1)
                        if following:
                            transposed_hi(c + 1, 1 - par, 0)

            transposed_hi(0, 0, 0)
            for k in range(KB):
                act.wait_ge(w1_in, 16 * KB)
                nc.scalar.copy(w1_hi[:, k, :, :], w1_f[:, k, :].rearrange("p (j m) -> p m j", m=MB)).then_inc(w1_hi_ready, 1)
                if k == 0:
                    transposed_hi(0, 0, 1)
            act.wait_ge(b1_in, 16)
            for m in range(MB):
                gelu(0, m, first=True)
                hidden_hi(0, m, first=True)
                if m == 0:
                    act.wait_ge(w2_in, 16)
                    nc.scalar.copy(w2_hi[:, :, :], w2_f[:, :, :]).then_inc(w2_hi_ready, 1)
                if m == 4:
                    act.wait_ge(counted, 1)
                    nc.scalar.activation(fr_ln[:], fr_cnt1[:], ACT.Ln).then_inc(logged, 1)
                    act.wait_ge(argued, 1)
                    nc.scalar.activation(wave[:, 3, :], wave[:, 2, :], ACT.Sin).then_inc(sined, 1)
                if m == 6:
                    transposed_hi(1, 1, 0)
                if m == 7:
                    transposed_hi(1, 1, 1)
            for k in range(KB):
                act.wait_ge(c_made, k + 1)
                nc.scalar.copy(c_f[:, k, :], p_c[:, k, 0:E]).then_inc(c_copied, 1)
            act.wait_ge(cw_made, 1)
            nc.scalar.copy(c_hi[:, :, E:CE], p_c[:, :, E:CE]).then_inc(cw_hi, 1)
            act.wait_ge(c_copied, KB)
            nc.scalar.copy(c_hi[:, :, 0:E], c_f[:, :, :]).then_inc(cw_hi, 1)

            with act.Fori(0, (CHUNKS - 2) // 2) as i:
                for u in range(2):
                    chunk(2 * i + 1 + u, 1 - u)
            chunk(CHUNKS - 1, 1, following=False)
            for q in range(PAIRS):
                corrected_copy(CHUNKS - 1, q)

        @block.vector
        def _(dve):
            dve.sem_inc(pair_out, PRIMED)
            links = [0]

            def then(ins):
                links[0] += 1
                ins.then_inc(link, 1)
                dve.wait_ge(link, links[0])

            def statistics(c, par):
                dve.wait_ge(x_in[par], 16 * (c // 2 + 1) if isinstance(c, int) else 8 * (c - par) + 16)
                for j in range(CT):
                    last = nc.vector.bn_stats(stats[:, j, :], x_chunk(c)[:, j, :])
                return last

            def x_chunk(c):
                return x_sb[:, bass.ds(c * CW, CW)].rearrange("p (j e) -> p j e", e=E)

            def aggregate(c, par):
                for j in range(CT):
                    last = nc.vector.bn_aggr(mv[par][:, j, :], stats[:, j, :])
                last.then_inc(stat_done, 1)

            def normalise(c, par):
                dve.wait_ge(rstd_done, c + 1)
                if not (isinstance(c, int) and c == 0):
                    dve.wait_ge(t_done, KB * c)
                for j in range(CT):
                    last = nc.vector.tensor_scalar(xn[:, j, :], x_chunk(c)[:, j, :], mv[par][:, j, 0:1],
                                                   rstd[par][:, j:j + 1], ALU.subtract, ALU.mult)
                last.then_inc(xn_done, 1)

            def transposed_lo(c, par, k):
                dve.wait_ge(t_hi, KB * c + k + 1)
                nc.vector.tensor_tensor(xT_lo[par][:, k, :], p_t[:], xT_hi[par][:, k, :].bitcast(F32),
                                        ALU.subtract).then_inc(t_lo, 1)

            def hidden_lo(c, m):
                dve.wait_ge(h_hi_done, MB * c + m + 1)
                nc.vector.tensor_tensor(h_lo[m % HR][:], h[m % 2][:], h_hi[m % HR][:].bitcast(F32),
                                        ALU.subtract).then_inc(h_lo_done, 1)

            def add_ffn(c):
                dve.wait_ge(down_done, MB * (c + 1))
                for q in range(PAIRS):
                    seg = x_chunk(c)[:, 2 * q:2 * q + 2, :]
                    nc.vector.tensor_tensor(seg, p_o[:, 2 * q:2 * q + 2, :], seg, ALU.add).then_inc(ffn_out, 1)

            def correct(c, q, hops):
                dve.wait_ge(wave_done, PAIRS * c + q + 1)
                lat = p_c[:, :, E:CE]
                bel = bel_sb[:, :].unsqueeze(1).broadcast_to([P, 2, LAT])
                pow2 = con[:, K_POW2:K_POW2 + LAT].unsqueeze(1).broadcast_to([P, 2, LAT])
                mask = mask_sb[:, :].unsqueeze(1).broadcast_to([P, 2, SYN])
                hops(nc.vector.scalar_tensor_tensor(out=bits[:], in0=lat, scalar=-1.0, in1=bel,
                                                    op0=ALU.mult, op1=ALU.is_lt))
                hops(nc.vector.tensor_tensor(weighed[:], bits[:], pow2, ALU.mult))
                with nc.allow_low_precision(reason="distinct powers of two under 2^24: an exact sum"):
                    summed = nc.vector.tensor_reduce(word[:], weighed[:], AX.X, ALU.add)
                hops(summed)
                hops(nc.vector.tensor_tensor(met[:], word[:].broadcast_to([P, 2, SYN]), mask, ALU.bitwise_and))
                hops(nc.vector.tensor_scalar(syn[:], met[:], 0.0, None, ALU.is_gt))
                hops(nc.vector.tensor_reduce(weight[:], syn[:], AX.X, ALU.add))
                hops(nc.vector.scalar_tensor_tensor(out=flips[:], in0=weight[:].broadcast_to([P, 2, SYN]),
                                                    scalar=3.0, in1=syn[:], op0=ALU.is_le, op1=ALU.mult))
                dve.wait_ge(cor_t, PRIMED + PAIRS * c + q)
                thrice = [P, 2, 3, SYN]
                nc.vector.tensor_tensor(cor[:, :, :, 0:SYN], bits[:, :, 0:SYN].unsqueeze(2).broadcast_to(thrice),
                                        flips[:].unsqueeze(2).broadcast_to(thrice), ALU.not_equal)
                nc.vector.tensor_copy(cor[:, :, :, SYN:LAT],
                                      bits[:, :, SYN:LAT].unsqueeze(2).broadcast_to(thrice)).then_inc(cor_done, 1)

            def add_wave(c, q):
                dve.wait_ge(le_done, PRIMED + PAIRS * c + q + 1)
                dve.wait_ge(ffn_out, PAIRS * (c + 1))
                seg = x_chunk(c)[:, 2 * q:2 * q + 2, :]
                nc.vector.tensor_tensor(seg, p_c[:, :, 0:E], seg, ALU.add).then_inc(pair_out, 1)

            def chunk(c, par, hops, following=True):
                add_ffn(c - 1)
                hidden_lo(c, 0)
                correct(c - 1, 0, hops)
                hidden_lo(c, 1)
                if following:
                    hops(statistics(c + 1, 1 - par))
                hidden_lo(c, 2)
                if following:
                    aggregate(c + 1, 1 - par)
                add_wave(c - 1, 0)
                hidden_lo(c, 3)
                if following:
                    normalise(c + 1, 1 - par)
                hidden_lo(c, 4)
                correct(c - 1, 1, hops)
                hidden_lo(c, 5)
                hidden_lo(c, 6)
                if following:
                    transposed_lo(c + 1, 1 - par, 0)
                    transposed_lo(c + 1, 1 - par, 1)
                hidden_lo(c, 7)
                add_wave(c - 1, 1)

            then(statistics(0, 0))
            aggregate(0, 0)
            dve.wait_ge(con_in, 16)
            nc.vector.tensor_copy(id_bf[:], con[:, K_ID:K_ID + P]).then_inc(id_ready, 1)
            normalise(0, 0)
            dve.wait_ge(fr_in, 16)
            for r in range(FR):
                last = nc.vector.bn_stats(fr_stats[:, r, :], fr_x[:, r, :])
            then(last)
            for r in range(FR):
                last = nc.vector.bn_aggr(fr_mv[:, r, :], fr_stats[:, r, :])
            last.then_inc(fr_stat, 1)
            transposed_lo(0, 0, 0)
            for k in range(KB):
                dve.wait_ge(w1_hi_ready, k + 1)
                nc.vector.tensor_tensor(w1_lo[:, k, :, :], w1_f[:, k, :].rearrange("p (j m) -> p m j", m=MB),
                                        w1_hi[:, k, :, :].bitcast(F32), ALU.subtract).then_inc(w1_ready, 1)
                if k == 0:
                    transposed_lo(0, 0, 1)
            hidden_lo(0, 0)
            dve.wait_ge(w2_hi_ready, 1)
            nc.vector.tensor_tensor(w2_lo[:, :, :], w2_f[:, :, :], w2_hi[:, :, :].bitcast(F32),
                                    ALU.subtract).then_inc(w2_ready, 1)
            hidden_lo(0, 1)
            dve.wait_ge(fr_rs, 1)
            for r in range(FR):
                last = nc.vector.tensor_scalar(fr_x[:, r, :], fr_x[:, r, :], fr_mv[:, r, 0:1], fr_rstd[:, r:r + 1],
                                               ALU.subtract, ALU.mult)
            then(last)
            fr_flat = fr_x[:, :, :].rearrange("p a e -> p (a e)")
            for k, n in enumerate(PREFIX):
                last = nc.vector.tensor_reduce(fr_sum[:, k:k + 1], fr_flat[:, 0:n], AX.X, ALU.add)
            then(last)
            then(nc.vector.tensor_tensor(fr_mean[:], fr_sum[:], con[:, K_INVN:K_INVN + 5], ALU.mult))
            hidden_lo(0, 2)
            for k, n in enumerate(PREFIX):
                then(nc.vector.tensor_scalar(fr_gt[:, 0:n], fr_flat[:, 0:n], fr_mean[:, k:k + 1], None,
                                             ALU.is_gt, ALU.add, accum_out=fr_cnt[:, k:k + 1]))
            nc.vector.tensor_scalar(fr_cnt1[:], fr_cnt[:], 1.0, None, ALU.max).then_inc(counted, 1)
            hidden_lo(0, 3)
            hidden_lo(0, 4)
            dve.wait_ge(logged, 1)
            then(nc.vector.tensor_tensor(fr_ly[:], fr_ln[:], con[:, K_COEF:K_COEF + 5], ALU.mult))
            then(nc.vector.tensor_reduce(fr_d[:, 0:1], fr_ly[:], AX.X, ALU.add))
            then(nc.vector.tensor_scalar(fr_d[:, 1:2], fr_d[:, 0:1], 1.0, 2.0, ALU.max, ALU.min))
            D, om, od, a, b = (fr_d[:, k:k + 1] for k in (1, 2, 3, 4, 5))
            then(nc.vector.tensor_scalar(om, D, 0.2, 1.0, ALU.mult, ALU.add))
            then(nc.vector.tensor_tensor(od, D, om, ALU.mult))
            then(nc.vector.tensor_scalar(a, D, 0.5, 1.0, ALU.mult, ALU.add))
            then(nc.vector.tensor_scalar(b, D, 0.1, None, ALU.mult))
            ka, ka2 = con[:, K_KA:K_KA + KB], con[:, K_KA2:K_KA2 + KB]
            then(nc.vector.tensor_scalar(wave[:, 0, 0:KB], ka, a, od, ALU.mult, ALU.add))
            then(nc.vector.tensor_scalar(wave[:, 0, KB:2 * KB], ka2, b, od, ALU.mult, ALU.add))
            then(nc.vector.tensor_tensor(wave[:, 1, KB:2 * KB], wave[:, 0, KB:2 * KB], ka, ALU.subtract))
            then(nc.vector.tensor_scalar(wave[:, 2, 0:KB], wave[:, 0, 0:KB], -1.0, math.pi, ALU.mult, ALU.add))
            nc.vector.tensor_scalar(wave[:, 2, KB:2 * KB], wave[:, 1, KB:2 * KB], -1.0, math.pi / 2,
                                    ALU.mult, ALU.add).then_inc(argued, 1)
            then(statistics(1, 1))
            aggregate(1, 1)
            dve.wait_ge(sined, 1)
            then(nc.vector.tensor_tensor(filt[:, 0, :], wave[:, 3, 0:KB], wave[:, 3, KB:2 * KB], ALU.mult))
            then(nc.vector.tensor_tensor(filt[:, 1, :], filt[:, 0, :], con[:, K_WK:K_WK + KB], ALU.mult))
            dve.wait_ge(basis_in, 16)
            for k in range(KB):
                nc.vector.tensor_scalar(basis_w[:, k, :], basis_sb[:, k, :], filt[:, 1, k:k + 1], None,
                                        ALU.mult).then_inc(basis_wd, 1)
            normalise(1, 1)
            hidden_lo(0, 5)
            hidden_lo(0, 6)
            transposed_lo(1, 1, 0)
            hidden_lo(0, 7)
            transposed_lo(1, 1, 1)
            then(nc.vector.memset(le3[:], 0.0))
            then(nc.vector.memset(cor[:], 0.0))
            nc.vector.memset(cor[:, :, :, LAT:LAT + 2], 1.0)
            dve.wait_ge(le_in, 48)
            then(nc.vector.tensor_copy(le3[0:ROWS_LE, :], le_f[:]))
            then(nc.vector.tensor_tensor(le_r1[:], le_f[:], le3[0:ROWS_LE, :], ALU.subtract))
            then(nc.vector.tensor_copy(le_mid[:], le_r1[:]))
            nc.vector.tensor_copy(le3[SEG:SEG + ROWS_LE, :], le_mid[:])
            nc.vector.tensor_tensor(le3[2 * SEG:2 * SEG + ROWS_LE, :], le_r1[:], le_mid[:],
                                    ALU.subtract).then_inc(le_ready, 1)
            dve.wait_ge(small_in, 48)
            dve.wait_ge(cw_hi, 1)
            nc.vector.tensor_tensor(c_lo[:, :, E:CE], p_c[:, :, E:CE], c_hi[:, :, E:CE].bitcast(F32), ALU.subtract)
            dve.wait_ge(cw_hi, 2)
            nc.vector.tensor_tensor(c_lo[:, :, 0:E], c_f[:, :, :], c_hi[:, :, 0:E].bitcast(F32),
                                    ALU.subtract).then_inc(c_ready, 1)

            base = links[0]
            per_chunk = 1 + 7 * PAIRS

            def hopper(start):
                n = [0]

                def hop(ins):
                    n[0] += 1
                    ins.then_inc(link, 1)
                    dve.wait_ge(link, start + n[0])
                return hop

            with dve.Fori(0, (CHUNKS - 2) // 2) as i:
                for u in range(2):
                    chunk(2 * i + 1 + u, 1 - u, hopper(i * (2 * per_chunk) + (base + u * per_chunk)))
            tail = hopper(base + (CHUNKS - 2) * per_chunk)
            chunk(CHUNKS - 1, 1, tail, following=False)
            add_ffn(CHUNKS - 1)
            for q in range(PAIRS):
                correct(CHUNKS - 1, q, tail)
                add_wave(CHUNKS - 1, q)

        @block.tensor
        def _(pe):
            pe.sem_inc(le_done, PRIMED)
            pe.sem_inc(cor_t, PRIMED)
            mm = nc.tensor.matmul

            def transpose_block(c, k):
                if k == 0:
                    pe.wait_ge(xn_done, c + 1)
                if not (isinstance(c, int) and c == 0 and k == 0):
                    pe.wait_ge(t_lo, KB * c + k)
                for j in range(CT):
                    last = nc.tensor.transpose(p_t[:, j * P:(j + 1) * P], xn[:, j, k * P:(k + 1) * P],
                                               con[:, K_ID:K_ID + P])
                last.then_inc(t_done, 1)

            def up(c, par, m, first=False):
                if m == 0:
                    pe.wait_ge(t_lo, KB * (c + 1))
                if not (first and m < 2):
                    pe.wait_ge(gelu_done, MB * c + m - 1)
                n = 0
                for w, xt in ((w1_hi, xT_hi), (w1_hi, xT_lo), (w1_lo, xT_hi)):
                    for k in range(KB):
                        last = mm(p_h[:, m % 2, :], w[:, k, m, :], xt[par][:, k, :],
                                  start=(n == 0), stop=(n == 3 * KB - 1))
                        n += 1
                last.then_inc(up_done, 1)

            def down(c, m, first=False):
                pe.wait_ge(h_lo_done, MB * c + m + 1)
                if m == 0 and not first:
                    pe.wait_ge(ffn_out, PAIRS * c)
                r = m % HR
                for j in range(CT):
                    tok = slice(j * P, (j + 1) * P)
                    for n, (hp, w) in enumerate(((h_hi, w2_hi), (h_hi, w2_lo), (h_lo, w2_hi))):
                        last = mm(p_o[:, j, :], hp[r][:, tok], w[:, m, :], start=(m == 0 and n == 0 and j % 2 == 0),
                                  stop=(m == MB - 1 and n == 2), skip_group_check=True)
                last.then_inc(down_done, 1)

            def wave_products(c, par, q):
                pe.wait_ge(pair_out, PRIMED + PAIRS * c + q)
                for r in range(2):
                    tok = slice((2 * q + r) * P, (2 * q + r + 1) * P)
                    n = 0
                    for k in range(KB):
                        for xt, cc in ((xT_hi, c_hi), (xT_hi, c_lo), (xT_lo, c_hi)):
                            last = mm(p_c[:, r, 0:CE], xt[par][:, k, tok], cc[:, k, :], start=(n == 0), stop=False,
                                      skip_group_check=True)
                            n += 1
                last.then_inc(wave_done, 1)

            def transpose_corrected(c, q):
                pe.wait_ge(cor_done, PAIRS * c + q + 1)
                pe.wait_ge(cor_sb, PRIMED + PAIRS * c + q)
                for r in range(2):
                    last = nc.tensor.transpose(p_g[0:3 * SEG, r * P:(r + 1) * P],
                                               cor[:, r, :, :].rearrange("p a s -> p (a s)"), id_bf[:])
                last.then_inc(cor_t, 1)

            def le_products(c, q):
                pe.wait_ge(cor_sb, PRIMED + PAIRS * c + q + 1)
                for r in range(2):
                    last = mm(p_c[:, r, 0:E], cor_T[:, r * P:(r + 1) * P], le3[:], start=False, stop=True,
                              skip_group_check=True)
                last.then_inc(le_done, 1)

            def chunk(c, par, following=True):
                for m in range(MB):
                    up(c, par, m)
                    if m == 0:
                        wave_products(c - 1, 1 - par, 0)
                    if m == 2:
                        transpose_corrected(c - 1, 0)
                    if m == 3:
                        le_products(c - 1, 0)
                    if m == 4:
                        wave_products(c - 1, 1 - par, 1)
                    if m == 6:
                        transpose_corrected(c - 1, 1)
                        if following:
                            transpose_block(c + 1, 0)
                    if m == 7:
                        le_products(c - 1, 1)
                        if following:
                            transpose_block(c + 1, 1)
                    if m >= 2:
                        down(c, m - 2)
                down(c, MB - 2)
                down(c, MB - 1)

            pe.wait_ge(con_in, 16)
            transpose_block(0, 0)
            transpose_block(0, 1)
            pe.wait_ge(w1_ready, KB)
            for m in range(MB):
                up(0, 0, m, first=True)
                if m >= 6:
                    transpose_block(1, m - 6)
                if m == 2:
                    pe.wait_ge(w2_ready, 1)
                if m >= 2:
                    down(0, m - 2, first=True)
            down(0, MB - 2)
            down(0, MB - 1)
            pe.wait_ge(basis_wd, KB)
            for i in range(KB):
                for k in range(KB):
                    last = mm(p_c[:, i, 0:E], basis_sb[:, k, i * P:(i + 1) * P], basis_w[:, k, :],
                              start=(k == 0), stop=(k == KB - 1))
                last.then_inc(c_made, 1)
            pe.wait_ge(c_copied, KB)
            pe.wait_ge(small_in, 48)
            for i in range(KB):
                for k in range(KB):
                    last = mm(p_c[:, i, E:CE], c_f[:, k, i * P:(i + 1) * P], wel_sb[:, k, :],
                              start=(k == 0), stop=(k == KB - 1))
            last.then_inc(cw_made, 1)
            pe.wait_ge(c_ready, 1)
            pe.wait_ge(id_ready, 1)
            pe.wait_ge(le_ready, 1)

            with pe.Fori(0, (CHUNKS - 2) // 2) as i:
                for u in range(2):
                    chunk(2 * i + 1 + u, 1 - u)
            chunk(CHUNKS - 1, 1, following=False)
            for q in range(PAIRS):
                wave_products(CHUNKS - 1, 1, q)
                transpose_corrected(CHUNKS - 1, q)
                le_products(CHUNKS - 1, q)


def constants():
    import numpy as np

    f4 = np.float32
    con = np.zeros((P, K_END), f4)
    con[:, K_ID:K_ID + P] = np.eye(P, dtype=f4)
    con[:, K_INVN:K_INVN + 5] = [1.0 / n for n in PREFIX]
    lx = np.log(np.array(SCALES, np.float64))
    n = len(SCALES)
    den = n * np.sum(lx * lx) - np.sum(lx) ** 2
    con[:, K_COEF:K_COEF + 5] = -(n * lx - np.sum(lx)) / den
    r = np.arange(E)
    freq = np.where(r <= E // 2, r, r - E // 2)
    ang = 2.0 * np.pi * ((freq[:, None] * r[None, :]) % E) / E
    basis = np.where((r <= E // 2)[:, None], np.cos(ang), np.sin(ang)).astype(f4)
    ka = (freq / E).astype(f4) + f4(1e-8)
    weight = np.where((r == 0) | (r == E // 2), 1.0, 2.0) / E
    by_block = lambda v: v.reshape(KB, P).T
    con[:, K_KA:K_KA + KB] = by_block(ka)
    con[:, K_KA2:K_KA2 + KB] = by_block(ka * ka)
    con[:, K_WK:K_WK + KB] = by_block(weight)
    con[:, K_POW2:K_POW2 + LAT] = 2.0 ** np.arange(LAT)
    a = np.array([[1, 1, 1, 0, 1, 1, 1, 0, 0, 0, 1, 1], [1, 1, 0, 1, 1, 1, 0, 0, 0, 1, 1, 0],
                  [1, 0, 1, 1, 1, 0, 0, 0, 1, 1, 0, 1], [0, 1, 1, 1, 0, 0, 0, 1, 1, 0, 1, 1],
                  [0, 0, 0, 0, 1, 1, 1, 1, 1, 1, 1, 1], [1, 1, 1, 1, 0, 0, 0, 0, 0, 0, 0, 0],
                  [0, 0, 0, 0, 1, 1, 1, 1, 0, 0, 0, 0], [1, 1, 0, 0, 1, 1, 0, 0, 1, 1, 0, 0],
                  [1, 0, 1, 0, 1, 0, 1, 0, 1, 0, 1, 0], [0, 1, 0, 1, 0, 1, 0, 1, 0, 1, 0, 1],
                  [1, 0, 0, 1, 1, 0, 0, 1, 1, 0, 0, 1], [0, 1, 1, 0, 0, 1, 1, 0, 0, 1, 1, 0]], np.int64)
    rows = np.concatenate([a.T, np.eye(SYN, dtype=np.int64)], axis=1)
    masks = np.tile((rows * 2 ** np.arange(LAT)).sum(axis=1).astype(np.int32), (P, 1))
    return con, basis, masks


_INS = ["L0_attn_x", "L0_attn_W_el", "L0_attn_b_el", "L0_attn_W_le", "L0_attn_b_le",
        "L0_ffn_w1", "L0_ffn_b1", "L0_ffn_w2", "L0_ffn_b2"]


def kernel(**inputs):
    import numpy as np
    import concourse.bacc as bacc
    from concourse.bass_utils import run_bass_kernel_spmd as run

    nc = bacc.Bacc("TRN2", target_bir_lowering=False, num_devices=1)
    arrays, args = {}, []
    for name in _INS:
        arrays[name] = np.ascontiguousarray(inputs[name])
    for name, a in zip(("consts", "basis", "masks"), constants()):
        arrays[name] = a
    for name, a in arrays.items():
        args.append(nc.dram_tensor(name, a.shape, mybir.dt.from_np(a.dtype), kind="ExternalInput").ap())
    out = nc.dram_tensor("out", (2, 4096, E), F32, kind="ExternalOutput").ap()
    build(nc, *args, out)
    r = run(nc, [arrays], core_ids=[0])
    return r.results[0]["out"]
```

```python
import math
from contextlib import ExitStack

import concourse.bass as bass
from concourse import mybir

F32, F32R, BF16, I32 = mybir.dt.float32, mybir.dt.float32r, mybir.dt.bfloat16, mybir.dt.int32
ALU = mybir.AluOpType
ACT = mybir.ActivationFunctionType
AX = mybir.AxisListType

P = 128
TOKENS, E, HID, LAT, SYN = 2 * 4096, 256, 1024, 24, 12
TILES = TOKENS // P
CT = 4
CTOK = CT * P
CHUNKS = TILES // CT
KB = E // P
MB = HID // P
PAIRS = CT // 2
CE = E + LAT
HR = 4
BANK = 512
W1_PARTS = ((0, 2), (2, 4), (4, MB))
W2_PARTS = ((0, 4), (4, MB))
SCALES = (2, 4, 8, 16, 32)
NS = len(SCALES)
PREFIX = [s * s for s in SCALES]
FR = max(PREFIX) // E
LN_EPS = 1e-5
SEG = 32
IDLE = 18
PRIMED = 1
ROWS_LE = LAT + 2

K_ID = 0
K_INVN = K_ID + P
K_COEF = K_INVN + 1
K_KA = K_COEF + P
K_KA2 = K_KA + KB
K_WK = K_KA2 + KB
K_POW2 = K_WK + KB
K_END = K_POW2 + LAT


def build(nc, x, w_el, b_el, w_le, b_le, w1, b1, w2, b2, consts, prefixes, basis, masks, out):
    ctx = ExitStack()
    with ctx:
        def sb(name, shape, dt):
            return ctx.enter_context(nc.sbuf_tensor(name, shape, dt))

        def ps(name, shape, dt):
            return ctx.enter_context(nc.psum_tensor(name, shape, dt))

        def sem(name):
            return ctx.enter_context(nc.semaphore(name))

        x_sb = sb("x_sb", [P, TILES * E], F32)
        xn = sb("xn", [P, CT, E], F32)
        xT_hi = [sb(f"xT_hi{i}", [P, KB, CTOK], F32R) for i in range(2)]
        xT_lo = [sb(f"xT_lo{i}", [P, KB, CTOK], F32R) for i in range(2)]
        h = [sb(f"h{i}", [P, CTOK], F32) for i in range(2)]
        h_hi = [sb(f"h_hi{i}", [P, CTOK], F32R) for i in range(HR)]
        h_lo = [sb(f"h_lo{i}", [P, CTOK], F32R) for i in range(HR)]
        w1_f = sb("w1_f", [P, KB, HID], F32)
        w1_hi = sb("w1_hi", [P, KB, HID], F32R)
        w1_lo = sb("w1_lo", [P, KB, HID], F32R)
        w2_f = sb("w2_f", [P, MB, E], F32)
        w2_hi = sb("w2_hi", [P, MB, E], F32R)
        w2_lo = sb("w2_lo", [P, MB, E], F32R)
        b1_sb = sb("b1_sb", [P, MB], F32)
        con = sb("con", [P, K_END], F32)
        mask_sb = sb("mask_sb", [P, SYN], I32)
        bel_sb = sb("bel_sb", [P, LAT], F32)
        wel_sb = sb("wel_sb", [P, KB, LAT], F32)
        basis_sb = sb("basis_sb", [P, KB, E], F32)
        basis_w = sb("basis_w", [P, KB, E], F32)
        c_f = sb("c_f", [P, E], F32)
        c_hi = sb("c_hi", [P, KB, CE], F32R)
        c_lo = sb("c_lo", [P, KB, CE], F32R)
        stats = sb("stats", [P, CT, 6], F32)
        mv = [sb(f"mv{i}", [P, CT, 2], F32) for i in range(2)]
        var_eps = sb("var_eps", [P, CT], F32)
        rstd = [sb(f"rstd{i}", [P, CT], F32) for i in range(2)]
        eps = sb("eps", [P, CT], F32)
        early = sb("early", [P, CT], F32)
        idle = sb("idle", [P, BANK], BF16)
        minus_half = sb("minus_half", [P, CT], F32)
        fr_x = sb("fr_x", [NS, FR, E], F32)
        fr_tab = sb("fr_tab", [NS, 3, FR * E], F32)
        fr_part = sb("fr_part", [NS, FR * E], F32)
        fr_stats = sb("fr_stats", [NS, FR, 6], F32)
        fr_mv = sb("fr_mv", [NS, FR, 2], F32)
        fr_ve = sb("fr_ve", [NS, FR], F32)
        fr_rstd = sb("fr_rstd", [NS, FR], F32)
        fr_sum = sb("fr_sum", [NS, 1], F32)
        fr_mean = sb("fr_mean", [NS, 1], F32)
        fr_cnt = sb("fr_cnt", [NS, 1], F32)
        fr_cnt1 = sb("fr_cnt1", [NS, 1], F32)
        fr_ln = sb("fr_ln", [NS, 1], F32)
        fr_d = sb("fr_d", [P, 8], F32)
        wave = sb("wave", [P, 4, 2 * KB], F32)
        filt = sb("filt", [P, 2, KB], F32)
        bits = sb("bits", [P, 2, LAT], F32)
        weighed = sb("weighed", [P, 2, LAT], F32)
        word = sb("word", [P, 2, 1], I32)
        met = sb("met", [P, 2, SYN], I32)
        syn = sb("syn", [P, 2, SYN], F32)
        weight = sb("weight", [P, 2, 1], F32)
        flips = sb("flips", [P, 2, SYN], F32)
        cor = sb("cor", [P, 2, 3, SEG], BF16)
        cor_T = sb("cor_T", [3 * SEG, 2 * P], BF16)
        id_bf = sb("id_bf", [P, P], BF16)
        le_f = sb("le_f", [ROWS_LE, E], F32)
        le_r1 = sb("le_r1", [ROWS_LE, E], F32)
        le_mid = sb("le_mid", [ROWS_LE, E], BF16)
        le3 = sb("le3", [3 * SEG, E], BF16)

        p_h = ps("p_h", [P, 2, BANK], F32)
        p_o = ps("p_o", [P, CT, E], F32)
        p_c = ps("p_c", [P, 2, BANK], F32)
        p_t = ps("p_t", [P, BANK], F32)
        p_g = ps("p_g", [P, 2 * BANK], BF16)

        x_in = [sem("x_even"), sem("x_odd")]
        x_head = sem("x_head")
        w1_in = [sem(f"w1_in{i}") for i in range(len(W1_PARTS))]
        w2_in = [sem(f"w2_in{i}") for i in range(len(W2_PARTS))]
        b1_in, con_in, fr_in = sem("b1_in"), sem("con_in"), sem("fr_in")
        basis_in, small_in, le_in = sem("basis_in"), sem("small_in"), sem("le_in")
        stored = sem("stored")
        idle_set = sem("idle_set")
        pool_set = sem("pool_set")
        id_ready = sem("id_ready")
        w1_hi_ready, w1_ready = sem("w1_hi_ready"), sem("w1_ready")
        w2_hi_ready, w2_ready = sem("w2_hi_ready"), sem("w2_ready")
        fr_stat, fr_veps, fr_rs = sem("fr_stat"), sem("fr_veps"), sem("fr_rs")
        logged, argued, sined = sem("logged"), sem("argued"), sem("sined")
        dim_made = sem("dim_made")
        basis_wd, c_made, c_copied = sem("basis_wd"), sem("c_made"), sem("c_copied")
        cw_made, c_hi_ready, c_ready = sem("cw_made"), sem("c_hi_ready"), sem("c_ready")
        le_ready = sem("le_ready")
        stat_done = sem("stat_done")
        veps_done, rstd_done = sem("veps_done"), sem("rstd_done")
        xn_done = sem("xn_done")
        t_done = sem("t_done")
        t_hi, t_lo = sem("t_hi"), sem("t_lo")
        up_done = sem("up_done")
        gelu_done, h_hi_done, h_lo_done = sem("gelu_done"), sem("h_hi_done"), sem("h_lo_done")
        down_done = sem("down_done")
        ffn_out = sem("ffn_out")
        wave_done = sem("wave_done")
        cor_done, cor_t, cor_sb = sem("cor_done"), sem("cor_t"), sem("cor_sb")
        le_done = sem("le_done")
        pair_out = sem("pair_out")
        link = sem("link")

        x_rows = x.rearrange("b s e -> (b s) e").rearrange("(p t) e -> p (t e)", p=P)
        out_rows = out.rearrange("b s e -> (b s) e").rearrange("(p t) e -> p (t e)", p=P)
        CW = CT * E
        block = ctx.enter_context(nc.Block())

        @block.sync
        def _(sp):
            for cols, arrived in ((slice(0, CW // 2), x_head), (slice(CW // 2, CW), x_in[0])):
                sp.dma_start(x_sb[:, cols], x_rows[:, cols]).then_inc(arrived, 16)
            def load_w1(n):
                cols = slice(W1_PARTS[n][0] * P, W1_PARTS[n][1] * P)
                sp.dma_start(w1_f[:, :, cols], w1[:, cols].rearrange("(k p) h -> p k h", p=P)).then_inc(w1_in[n], 16)

            def load_w2(n):
                m0, m1 = W2_PARTS[n]
                sp.dma_start(w2_f[:, m0:m1, :],
                             w2[m0 * P:m1 * P, :].rearrange("(m p) e -> p m e", p=P)).then_inc(w2_in[n], 16)

            sp.dma_start(con[:], consts).then_inc(con_in, 16)
            load_w1(0)
            load_w1(1)
            load_w2(0)
            with nc.allow_non_contiguous_dma(reason="4 KB once"):
                sp.dma_start(b1_sb[:], b1.rearrange("(m p) -> p m", p=P)).then_inc(b1_in, 16)
            load_w1(2)
            sp.dma_start(fr_x[:, :, :].rearrange("p a e -> p (a e)"),
                         x[0, 0:FR, :].rearrange("a e -> (a e)").partition_broadcast(NS)).then_inc(fr_in, 16)
            sp.dma_start(fr_tab[:, :, :], prefixes).then_inc(fr_in, 16)
            sp.dma_start(x_sb[:, CW:2 * CW], x_rows[:, CW:2 * CW]).then_inc(x_in[1], 16)
            load_w2(1)
            sp.dma_start(basis_sb[:, :, :], basis.rearrange("(k p) e -> p k e", p=P)).then_inc(basis_in, 16)
            sp.dma_start(wel_sb[:, :, :], w_el.rearrange("(k p) l -> p k l", p=P)).then_inc(small_in, 16)
            sp.dma_start(mask_sb[:], masks).then_inc(small_in, 16)
            sp.dma_start(bel_sb[:], b_el.partition_broadcast(P)).then_inc(small_in, 16)
            sp.dma_start(le_f[0:LAT, :], w_le).then_inc(le_in, 16)
            sp.dma_start(le_f[LAT:LAT + 1, :], b_le[None, :]).then_inc(le_in, 16)
            sp.dma_start(le_f[LAT + 1:LAT + 2, :], b2[None, :]).then_inc(le_in, 16)
            with sp.Fori(1, CHUNKS // 2) as i:
                for par in range(2):
                    sp.wait_ge(x_in[par], i * 16)
                    at = i * (2 * CW) + par * CW
                    sp.dma_start(x_sb[:, bass.ds(at, CW)], x_rows[:, bass.ds(at, CW)]).then_inc(x_in[par], 16)
            with sp.Fori(0, CHUNKS * PAIRS) as n:
                sp.wait_ge(pair_out, PRIMED + n + 1)
                sp.dma_start(out_rows[:, bass.ds(n * (2 * E), 2 * E)],
                             x_sb[:, bass.ds(n * (2 * E), 2 * E)]).then_inc(stored, 16)
            sp.wait_ge(stored, 16 * CHUNKS * PAIRS)

        @block.gpsimd
        def _(pool):
            nc.gpsimd.memset(eps[:], LN_EPS).then_inc(pool_set, 1)
            nc.gpsimd.memset(minus_half[:], -0.5).then_inc(pool_set, 1)
            pool.wait_ge(pool_set, 2)

            def inverse_root(c, par):
                pool.wait_ge(stat_done, c + 1)
                nc.gpsimd.tensor_tensor(var_eps[:], mv[par][:, :, 1], eps[:], ALU.add).then_inc(veps_done, 1)
                pool.wait_ge(veps_done, c + 1)
                nc.gpsimd.tensor_tensor(rstd[par][:], var_eps[:], minus_half[:], ALU.pow).then_inc(rstd_done, 1)

            inverse_root(0, 0)
            pool.wait_ge(fr_stat, 1)
            nc.gpsimd.tensor_tensor(fr_ve[:], fr_mv[:, :, 1], eps[0:NS, :], ALU.add).then_inc(fr_veps, 1)
            pool.wait_ge(fr_veps, 1)
            nc.gpsimd.tensor_tensor(fr_rstd[:], fr_ve[:], minus_half[0:NS, :], ALU.pow).then_inc(fr_rs, 1)
            cols = slice(W1_PARTS[2][0] * P, W1_PARTS[2][1] * P)
            pool.wait_ge(w1_hi_ready, 3)
            nc.gpsimd.tensor_tensor(w1_lo[:, :, cols], w1_f[:, :, cols], w1_hi[:, :, cols].bitcast(F32),
                                    ALU.subtract).then_inc(w1_ready, 1)
            inverse_root(1, 1)
            m0, m1 = W2_PARTS[1]
            pool.wait_ge(w2_hi_ready, 2)
            nc.gpsimd.tensor_tensor(w2_lo[:, m0:m1, :], w2_f[:, m0:m1, :], w2_hi[:, m0:m1, :].bitcast(F32),
                                    ALU.subtract).then_inc(w2_ready, 1)
            with pool.Fori(0, (CHUNKS - 2) // 2) as i:
                for u in range(2):
                    inverse_root(2 * i + 2 + u, u)

        @block.scalar
        def _(act):
            act.sem_inc(cor_sb, PRIMED)
            act.wait_ge(pool_set, 2)
            nc.scalar.activation(early[:], eps[:], ACT.Gelu)

            def transposed_hi(c, par, k, bank=p_t):
                act.wait_ge(t_done, KB * c + k + 1)
                nc.scalar.copy(xT_hi[par][:, k, :], bank[:]).then_inc(t_hi, 1)

            def gelu(c, m, first=False):
                act.wait_ge(up_done, MB * c + m + 1)
                if not (first and m < 2):
                    act.wait_ge(h_lo_done, MB * c + m - 1)
                nc.scalar.activation(h[m % 2][:], p_h[:, m % 2, :], ACT.Gelu,
                                     bias=b1_sb[:, m:m + 1]).then_inc(gelu_done, 1)

            def hidden_hi(c, m, first=False):
                act.wait_ge(gelu_done, MB * c + m + 1)
                if not (first and m < HR):
                    act.wait_ge(down_done, MB * c + m + 1 - HR)
                nc.scalar.copy(h_hi[m % HR][:], h[m % 2][:]).then_inc(h_hi_done, 1)

            def corrected_copy(c, q):
                act.wait_ge(cor_t, PRIMED + PAIRS * c + q + 1)
                act.wait_ge(le_done, PRIMED + PAIRS * c + q)
                nc.scalar.copy(cor_T[:], p_g[0:3 * SEG, 0:2 * P]).then_inc(cor_sb, 1)

            def chunk(c, par, wave=True, following=True):
                for m in range(MB):
                    gelu(c, m)
                    if m == MB - 1 and following:
                        transposed_hi(c + 1, 1 - par, 1)
                    hidden_hi(c, m)
                    if m == 3:
                        corrected_copy(c - 1, 0)
                    if m == 6 and following:
                        transposed_hi(c + 1, 1 - par, 0)
                corrected_copy(c - 1, 1)

            def w1_part_hi(n):
                cols = slice(W1_PARTS[n][0] * P, W1_PARTS[n][1] * P)
                act.wait_ge(w1_in[n], 16)
                nc.scalar.copy(w1_hi[:, :, cols], w1_f[:, :, cols]).then_inc(w1_hi_ready, 1)

            def w2_part_hi(n):
                m0, m1 = W2_PARTS[n]
                act.wait_ge(w2_in[n], 16)
                nc.scalar.copy(w2_hi[:, m0:m1, :], w2_f[:, m0:m1, :]).then_inc(w2_hi_ready, 1)

            w1_part_hi(0)
            act.wait_ge(con_in, 16)
            nc.scalar.copy(id_bf[:], con[:, K_ID:K_ID + P]).then_inc(id_ready, 1)
            for k in range(KB):
                transposed_hi(0, 0, k, p_c[:, k, :])
            w1_part_hi(1)
            w2_part_hi(0)
            act.wait_ge(b1_in, 16)
            for m in range(MB):
                gelu(0, m, first=True)
                hidden_hi(0, m, first=True)
                if m == 0:
                    w1_part_hi(2)
                if m == 1:
                    w2_part_hi(1)
                if m == 6:
                    act.wait_ge(argued, 1)
                    nc.scalar.activation(wave[:, 3, :], wave[:, 2, :], ACT.Sin).then_inc(sined, 1)
                if m >= 6:
                    transposed_hi(1, 1, m - 6)
            act.wait_ge(c_copied, 1)
            nc.scalar.copy(c_hi[:, 0, 0:E], c_f[:])
            nc.scalar.copy(c_hi[:, 1, 0:P], c_f[:, P:E])
            nc.scalar.copy(c_hi[:, 1, P:E], c_f[:, 0:P])
            act.wait_ge(cw_made, 1)
            nc.scalar.copy(c_hi[:, :, E:CE], p_c[:, :, E:CE]).then_inc(c_hi_ready, 1)

            with act.Fori(0, (CHUNKS - 2) // 2) as i:
                for u in range(2):
                    chunk(2 * i + 1 + u, 1 - u)
            chunk(CHUNKS - 1, 1, following=False)
            for q in range(PAIRS):
                corrected_copy(CHUNKS - 1, q)

        @block.vector
        def _(dve):
            dve.sem_inc(pair_out, PRIMED)
            nc.vector.memset(idle[:], 0.0).then_inc(idle_set, 1)
            links = [0]

            def then(ins):
                links[0] += 1
                ins.then_inc(link, 1)
                dve.wait_ge(link, links[0])

            def statistics(c, par):
                first = isinstance(c, int) and c == 0
                if first:
                    dve.wait_ge(x_head, 16)
                for j in range(CT):
                    if j == (CT // 2 if first else 0):
                        dve.wait_ge(x_in[par], 8 * (c - par) + 16)
                    last = nc.vector.bn_stats(stats[:, j, :], x_chunk(c)[:, j, :])
                return last

            def x_chunk(c):
                return x_sb[:, bass.ds(c * CW, CW)].rearrange("p (j e) -> p j e", e=E)

            def aggregate(c, par):
                for j in range(CT):
                    last = nc.vector.bn_aggr(mv[par][:, j, :], stats[:, j, :])
                last.then_inc(stat_done, 1)

            def normalise(c, par):
                dve.wait_ge(rstd_done, c + 1)
                if not (isinstance(c, int) and c == 0):
                    dve.wait_ge(t_done, KB * c)
                for j in range(CT):
                    last = nc.vector.tensor_scalar(xn[:, j, :], x_chunk(c)[:, j, :], mv[par][:, j, 0:1],
                                                   rstd[par][:, j:j + 1], ALU.subtract, ALU.mult)
                last.then_inc(xn_done, 1)

            def transposed_lo(c, par, k, bank=p_t):
                dve.wait_ge(t_hi, KB * c + k + 1)
                nc.vector.tensor_tensor(xT_lo[par][:, k, :], bank[:], xT_hi[par][:, k, :].bitcast(F32),
                                        ALU.subtract).then_inc(t_lo, 1)

            def hidden_lo(c, m):
                dve.wait_ge(h_hi_done, MB * c + m + 1)
                nc.vector.tensor_tensor(h_lo[m % HR][:], h[m % 2][:], h_hi[m % HR][:].bitcast(F32),
                                        ALU.subtract).then_inc(h_lo_done, 1)

            def add_ffn(c):
                dve.wait_ge(down_done, MB * (c + 1))
                for q in range(PAIRS):
                    seg = x_chunk(c)[:, 2 * q:2 * q + 2, :]
                    nc.vector.tensor_tensor(seg, p_o[:, 2 * q:2 * q + 2, :], seg, ALU.add).then_inc(ffn_out, 1)

            def correct(c, q, hops, banks=p_c):
                dve.wait_ge(wave_done, PAIRS * c + q + 1)
                lat = banks[:, :, E:CE]
                bel = bel_sb[:, :].unsqueeze(1).broadcast_to([P, 2, LAT])
                pow2 = con[:, K_POW2:K_POW2 + LAT].unsqueeze(1).broadcast_to([P, 2, LAT])
                mask = mask_sb[:, :].unsqueeze(1).broadcast_to([P, 2, SYN])
                hops(nc.vector.scalar_tensor_tensor(out=bits[:], in0=lat, scalar=-1.0, in1=bel,
                                                    op0=ALU.mult, op1=ALU.is_lt))
                hops(nc.vector.tensor_tensor(weighed[:], bits[:], pow2, ALU.mult))
                with nc.allow_low_precision(reason="distinct powers of two under 2^24: an exact sum"):
                    summed = nc.vector.tensor_reduce(word[:], weighed[:], AX.X, ALU.add)
                hops(summed)
                hops(nc.vector.tensor_tensor(met[:], word[:].broadcast_to([P, 2, SYN]), mask, ALU.bitwise_and))
                hops(nc.vector.tensor_scalar(syn[:], met[:], 0.0, None, ALU.is_gt))
                hops(nc.vector.tensor_reduce(weight[:], syn[:], AX.X, ALU.add))
                hops(nc.vector.scalar_tensor_tensor(out=flips[:], in0=weight[:].broadcast_to([P, 2, SYN]),
                                                    scalar=3.0, in1=syn[:], op0=ALU.is_le, op1=ALU.mult))
                dve.wait_ge(cor_t, PRIMED + PAIRS * c + q)
                thrice = [P, 2, 3, SYN]
                nc.vector.tensor_tensor(cor[:, :, :, 0:SYN], bits[:, :, 0:SYN].unsqueeze(2).broadcast_to(thrice),
                                        flips[:].unsqueeze(2).broadcast_to(thrice), ALU.not_equal)
                nc.vector.tensor_copy(cor[:, :, :, SYN:LAT],
                                      bits[:, :, SYN:LAT].unsqueeze(2).broadcast_to(thrice)).then_inc(cor_done, 1)

            def add_wave(c, q, banks=p_c):
                dve.wait_ge(le_done, PRIMED + PAIRS * c + q + 1)
                dve.wait_ge(ffn_out, PAIRS * (c + 1))
                seg = x_chunk(c)[:, 2 * q:2 * q + 2, :]
                nc.vector.tensor_tensor(seg, banks[:, :, 0:E], seg, ALU.add).then_inc(pair_out, 1)

            def chunk(c, par, hops, following=True):
                add_ffn(c - 1)
                hidden_lo(c, 0)
                if following:
                    hops(statistics(c + 1, 1 - par))
                hidden_lo(c, 1)
                if following:
                    aggregate(c + 1, 1 - par)
                correct(c - 1, 0, hops)
                hidden_lo(c, 2)
                hidden_lo(c, 3)
                if following:
                    normalise(c + 1, 1 - par)
                add_wave(c - 1, 0)
                hidden_lo(c, 4)
                hidden_lo(c, 5)
                correct(c - 1, 1, hops)
                hidden_lo(c, 6)
                if following:
                    transposed_lo(c + 1, 1 - par, 0)
                    transposed_lo(c + 1, 1 - par, 1)
                hidden_lo(c, 7)
                add_wave(c - 1, 1)

            def w1_part_lo(n):
                cols = slice(W1_PARTS[n][0] * P, W1_PARTS[n][1] * P)
                dve.wait_ge(w1_hi_ready, n + 1)
                nc.vector.tensor_tensor(w1_lo[:, :, cols], w1_f[:, :, cols], w1_hi[:, :, cols].bitcast(F32),
                                        ALU.subtract).then_inc(w1_ready, 1)

            def w2_part_lo(n):
                m0, m1 = W2_PARTS[n]
                dve.wait_ge(w2_hi_ready, n + 1)
                nc.vector.tensor_tensor(w2_lo[:, m0:m1, :], w2_f[:, m0:m1, :], w2_hi[:, m0:m1, :].bitcast(F32),
                                        ALU.subtract).then_inc(w2_ready, 1)

            then(statistics(0, 0))
            aggregate(0, 0)
            normalise(0, 0)
            w1_part_lo(0)
            for k in range(KB):
                transposed_lo(0, 0, k, p_c[:, k, :])
            w1_part_lo(1)
            w2_part_lo(0)
            dve.wait_ge(fr_in, 32)
            for r in range(FR):
                last = nc.vector.bn_stats(fr_stats[:, r, :], fr_x[:, r, :])
            then(last)
            for r in range(FR):
                last = nc.vector.bn_aggr(fr_mv[:, r, :], fr_stats[:, r, :])
            last.then_inc(fr_stat, 1)
            hidden_lo(0, 0)
            then(statistics(1, 1))
            aggregate(1, 1)
            hidden_lo(0, 1)
            dve.wait_ge(fr_rs, 1)
            for r in range(FR):
                last = nc.vector.tensor_scalar(fr_x[:, r, :], fr_x[:, r, :], fr_mv[:, r, 0:1], fr_rstd[:, r:r + 1],
                                               ALU.subtract, ALU.mult)
            then(last)
            hidden_lo(0, 2)
            fr_flat = fr_x[:, :, :].rearrange("p a e -> p (a e)")
            then(nc.vector.scalar_tensor_tensor(out=fr_part[:], in0=fr_flat, scalar=1.0, in1=fr_tab[:, 0, :],
                                                op0=ALU.mult, op1=ALU.mult, accum_out=fr_sum[:]))
            then(nc.vector.tensor_scalar(fr_mean[:], fr_sum[:], con[0:NS, K_INVN:K_INVN + 1], None, ALU.mult))
            hidden_lo(0, 3)
            then(nc.vector.scalar_tensor_tensor(out=fr_part[:], in0=fr_flat, scalar=fr_mean[:, 0:1],
                                                in1=fr_tab[:, 0, :], op0=ALU.is_gt, op1=ALU.mult,
                                                accum_out=fr_cnt[:]))
            then(nc.vector.tensor_scalar(fr_cnt1[:], fr_cnt[:], 1.0, None, ALU.max))
            hidden_lo(0, 4)
            nc.vector.scalar_tensor_tensor(out=fr_part[:], in0=fr_tab[:, 1, :], scalar=fr_cnt1[:, 0:1],
                                           in1=fr_tab[:, 2, :], op0=ALU.is_equal, op1=ALU.mult,
                                           accum_out=fr_ln[:]).then_inc(logged, 1)
            normalise(1, 1)
            dve.wait_ge(dim_made, 1)
            then(nc.vector.tensor_scalar(fr_d[:, 1:2], p_c[:, 0, 0:1], 1.0, 2.0, ALU.max, ALU.min))
            D, om, od, a, b = (fr_d[:, k:k + 1] for k in (1, 2, 3, 4, 5))
            then(nc.vector.tensor_scalar(om, D, 0.2, 1.0, ALU.mult, ALU.add))
            nc.vector.tensor_scalar(a, D, 0.5, 1.0, ALU.mult, ALU.add)
            nc.vector.tensor_scalar(b, D, 0.1, None, ALU.mult)
            then(nc.vector.tensor_tensor(od, D, om, ALU.mult))
            ka, ka2 = con[:, K_KA:K_KA + KB], con[:, K_KA2:K_KA2 + KB]
            nc.vector.tensor_scalar(wave[:, 0, 0:KB], ka, a, od, ALU.mult, ALU.add)
            then(nc.vector.tensor_scalar(wave[:, 0, KB:2 * KB], ka2, b, od, ALU.mult, ALU.add))
            then(nc.vector.tensor_tensor(wave[:, 1, KB:2 * KB], wave[:, 0, KB:2 * KB], ka, ALU.subtract))
            then(nc.vector.tensor_scalar(wave[:, 2, 0:KB], wave[:, 0, 0:KB], -1.0, math.pi, ALU.mult, ALU.add))
            nc.vector.tensor_scalar(wave[:, 2, KB:2 * KB], wave[:, 1, KB:2 * KB], -1.0, math.pi / 2,
                                    ALU.mult, ALU.add).then_inc(argued, 1)
            hidden_lo(0, 5)
            hidden_lo(0, 6)
            dve.wait_ge(sined, 1)
            then(nc.vector.tensor_tensor(filt[:, 0, :], wave[:, 3, 0:KB], wave[:, 3, KB:2 * KB], ALU.mult))
            then(nc.vector.tensor_tensor(filt[:, 1, :], filt[:, 0, :], con[:, K_WK:K_WK + KB], ALU.mult))
            dve.wait_ge(basis_in, 16)
            for k in range(KB):
                nc.vector.tensor_scalar(basis_w[:, k, :], basis_sb[:, k, :], filt[:, 1, k:k + 1], None,
                                        ALU.mult).then_inc(basis_wd, 1)
            transposed_lo(1, 1, 0)
            dve.wait_ge(c_made, 1)
            nc.vector.tensor_copy(c_f[:], p_c[:, 0, 0:E]).then_inc(c_copied, 1)
            hidden_lo(0, 7)
            transposed_lo(1, 1, 1)
            dve.wait_ge(small_in, 48)
            dve.wait_ge(c_hi_ready, 1)
            nc.vector.tensor_tensor(c_lo[:, 0, 0:E], c_f[:], c_hi[:, 0, 0:E].bitcast(F32), ALU.subtract)
            nc.vector.tensor_tensor(c_lo[:, 1, 0:P], c_f[:, P:E], c_hi[:, 1, 0:P].bitcast(F32), ALU.subtract)
            nc.vector.tensor_tensor(c_lo[:, 1, P:E], c_f[:, 0:P], c_hi[:, 1, P:E].bitcast(F32), ALU.subtract)
            nc.vector.tensor_tensor(c_lo[:, :, E:CE], p_c[:, :, E:CE], c_hi[:, :, E:CE].bitcast(F32),
                                    ALU.subtract).then_inc(c_ready, 1)

            then(nc.vector.memset(le3[:], 0.0))
            then(nc.vector.memset(cor[:], 0.0))
            nc.vector.memset(cor[:, :, :, LAT:LAT + 2], 1.0)
            dve.wait_ge(le_in, 48)
            then(nc.vector.tensor_copy(le3[0:ROWS_LE, :], le_f[:]))
            then(nc.vector.tensor_tensor(le_r1[:], le_f[:], le3[0:ROWS_LE, :], ALU.subtract))
            then(nc.vector.tensor_copy(le_mid[:], le_r1[:]))
            nc.vector.tensor_copy(le3[SEG:SEG + ROWS_LE, :], le_mid[:])
            nc.vector.tensor_tensor(le3[2 * SEG:2 * SEG + ROWS_LE, :], le_r1[:], le_mid[:],
                                    ALU.subtract).then_inc(le_ready, 1)
            base = links[0]
            per_chunk = 1 + 7 * PAIRS

            def hopper(start):
                n = [0]

                def hop(ins):
                    n[0] += 1
                    ins.then_inc(link, 1)
                    dve.wait_ge(link, start + n[0])
                return hop

            with dve.Fori(0, (CHUNKS - 2) // 2) as i:
                for u in range(2):
                    chunk(2 * i + 1 + u, 1 - u, hopper(i * (2 * per_chunk) + (base + u * per_chunk)))
            tail = hopper(base + (CHUNKS - 2) * per_chunk)
            chunk(CHUNKS - 1, 1, tail, following=False)
            for q, banks in enumerate((p_h, p_c)):
                dve.wait_ge(cor_done, PAIRS * (CHUNKS - 1) + q)
                correct(CHUNKS - 1, q, tail, banks)
            add_ffn(CHUNKS - 1)
            for q, banks in enumerate((p_h, p_c)):
                add_wave(CHUNKS - 1, q, banks)

        @block.tensor
        def _(pe):
            pe.sem_inc(le_done, PRIMED)
            pe.sem_inc(cor_t, PRIMED)
            mm = nc.tensor.matmul

            def transpose_block(c, k, bank=p_t):
                if k == 0:
                    pe.wait_ge(xn_done, c + 1)
                if bank is p_t:
                    pe.wait_ge(t_lo, KB * c + k)
                for j in range(CT):
                    last = nc.tensor.transpose(bank[:, j * P:(j + 1) * P], xn[:, j, k * P:(k + 1) * P],
                                               con[:, K_ID:K_ID + P])
                last.then_inc(t_done, 1)

            def up(c, par, m, first=False):
                if m == 0:
                    pe.wait_ge(t_lo, KB * (c + 1))
                for n, (m0, _) in enumerate(W1_PARTS):
                    if first and m == m0:
                        pe.wait_ge(w1_ready, n + 1)
                if not (first and m < 2):
                    pe.wait_ge(gelu_done, MB * c + m - 1)
                n = 0
                for w, xt in ((w1_hi, xT_hi), (w1_hi, xT_lo), (w1_lo, xT_hi)):
                    for k in range(KB):
                        last = mm(p_h[:, m % 2, :], w[:, k, m * P:(m + 1) * P], xt[par][:, k, :],
                                  start=(n == 0), stop=(n == 3 * KB - 1))
                        n += 1
                last.then_inc(up_done, 1)

            def down(c, m, first=False):
                pe.wait_ge(h_lo_done, MB * c + m + 1)
                if m == 0 and not first:
                    pe.wait_ge(ffn_out, PAIRS * c)
                for n, (m0, _) in enumerate(W2_PARTS):
                    if first and m == m0:
                        pe.wait_ge(w2_ready, n + 1)
                r = m % HR
                for j in range(CT):
                    tok = slice(j * P, (j + 1) * P)
                    for n, (hp, w) in enumerate(((h_hi, w2_hi), (h_hi, w2_lo), (h_lo, w2_hi))):
                        last = mm(p_o[:, j, :], hp[r][:, tok], w[:, m, :], start=(m == 0 and n == 0 and j % 2 == 0),
                                  stop=(m == MB - 1 and n == 2), skip_group_check=True)
                last.then_inc(down_done, 1)

            def wave_products(c, par, q, banks=p_c, user=None):
                if banks is p_c:
                    pe.wait_ge(pair_out, PRIMED + (PAIRS * c + q if user is None else user + 1))
                else:
                    pe.wait_ge(gelu_done, MB * (c + 1))
                pe.wait_ge(c_ready, 1)
                for r in range(2):
                    tok = slice((2 * q + r) * P, (2 * q + r + 1) * P)
                    n = 0
                    for k in range(KB):
                        for xt, cc in ((xT_hi, c_hi), (xT_hi, c_lo), (xT_lo, c_hi)):
                            last = mm(banks[:, r, 0:CE], xt[par][:, k, tok], cc[:, k, :], start=(n == 0), stop=False,
                                      skip_group_check=True)
                            n += 1
                last.then_inc(wave_done, 1)

            def transpose_corrected(c, q):
                pe.wait_ge(cor_done, PAIRS * c + q + 1)
                pe.wait_ge(cor_sb, PRIMED + PAIRS * c + q)
                for r in range(2):
                    last = nc.tensor.transpose(p_g[0:3 * SEG, r * P:(r + 1) * P],
                                               cor[:, r, :, :].rearrange("p a s -> p (a s)"), id_bf[:])
                last.then_inc(cor_t, 1)

            def le_products(c, q, banks=p_c):
                pe.wait_ge(cor_sb, PRIMED + PAIRS * c + q + 1)
                pe.wait_ge(le_ready, 1)
                for r in range(2):
                    last = mm(banks[:, r, 0:E], cor_T[:, r * P:(r + 1) * P], le3[:], start=False, stop=True,
                              skip_group_check=True)
                last.then_inc(le_done, 1)

            def chunk(c, par, following=True):
                for m in range(MB):
                    up(c, par, m)
                    if m == 1:
                        wave_products(c - 1, 1 - par, 0)
                    if m == 4:
                        le_products(c - 1, 0)
                    if m == 5:
                        wave_products(c - 1, 1 - par, 1)
                    if m >= 6 and following:
                        transpose_block(c + 1, m - 6)
                    if m == 7:
                        transpose_corrected(c - 1, 1)
                    if m >= 2:
                        down(c, m - 2)
                    if m == 3:
                        transpose_corrected(c - 1, 0)
                if following:
                    down(c, MB - 2)
                    le_products(c - 1, 1)
                else:
                    le_products(c - 1, 1)
                    down(c, MB - 2)
                    wave_products(c, par, 0, p_h)
                    wave_products(c, par, 1, p_c, user=PAIRS * c - 1)
                down(c, MB - 1)
                if not following:
                    for q, banks in enumerate((p_h, p_c)):
                        transpose_corrected(c, q)
                        le_products(c, q, banks)

            def circulant():
                pe.wait_ge(basis_wd, KB)
                for k in range(KB):
                    last = mm(p_c[:, 0, 0:E], basis_sb[:, k, 0:P], basis_w[:, k, :], start=(k == 0), stop=(k == KB - 1))
                last.then_inc(c_made, 1)

            def latent_products():
                pe.wait_ge(c_copied, 1)
                pe.wait_ge(small_in, 48)
                for i in range(KB):
                    for k in range(KB):
                        ab = c_f[:, P:E] if i != k else c_f[:, 0:P]
                        last = mm(p_c[:, i, E:CE], ab, wel_sb[:, k, :], start=(k == 0), stop=(k == KB - 1))
                last.then_inc(cw_made, 1)

            pe.wait_ge(idle_set, 1)
            for _ in range(IDLE):
                mm(p_o[:, 0:2, :], idle[:, 0:P], idle[:], start=True, stop=True)
            pe.wait_ge(con_in, 16)
            for k in range(KB):
                transpose_block(0, k, p_c[:, k, :])
            for m in range(MB):
                if m == 6:
                    pe.wait_ge(logged, 1)
                    mm(p_c[:, 0, 0:1], con[0:NS, K_COEF:K_COEF + P], fr_ln[:], start=True, stop=True).then_inc(dim_made, 1)
                up(0, 0, m, first=True)
                if m >= 6:
                    transpose_block(1, m - 6)
                if m >= 2:
                    down(0, m - 2, first=True)
                if m == 7:
                    circulant()
            down(0, MB - 2)
            latent_products()
            down(0, MB - 1)
            pe.wait_ge(id_ready, 1)

            with pe.Fori(0, (CHUNKS - 2) // 2) as i:
                for u in range(2):
                    chunk(2 * i + 1 + u, 1 - u)
            chunk(CHUNKS - 1, 1, following=False)


def constants():
    import numpy as np

    f4 = np.float32
    con = np.zeros((P, K_END), f4)
    con[:, K_ID:K_ID + P] = np.eye(P, dtype=f4)
    con[0:NS, K_INVN] = [1.0 / n for n in PREFIX]
    lx = np.log(np.array(SCALES, np.float64))
    n = len(SCALES)
    den = n * np.sum(lx * lx) - np.sum(lx) ** 2
    con[0:NS, K_COEF:K_COEF + P] = (-(n * lx - np.sum(lx)) / den)[:, None]
    r = np.arange(E)
    freq = np.where(r <= E // 2, r, r - E // 2)
    ang = 2.0 * np.pi * ((freq[:, None] * r[None, :]) % E) / E
    basis = np.where((r <= E // 2)[:, None], np.cos(ang), np.sin(ang)).astype(f4)
    ka = (freq / E).astype(f4) + f4(1e-8)
    weight = np.where((r == 0) | (r == E // 2), 1.0, 2.0) / E
    by_block = lambda v: v.reshape(KB, P).T
    con[:, K_KA:K_KA + KB] = by_block(ka)
    con[:, K_KA2:K_KA2 + KB] = by_block(ka * ka)
    con[:, K_WK:K_WK + KB] = by_block(weight)
    con[:, K_POW2:K_POW2 + LAT] = 2.0 ** np.arange(LAT)
    a = np.array([[1, 1, 1, 0, 1, 1, 1, 0, 0, 0, 1, 1], [1, 1, 0, 1, 1, 1, 0, 0, 0, 1, 1, 0],
                  [1, 0, 1, 1, 1, 0, 0, 0, 1, 1, 0, 1], [0, 1, 1, 1, 0, 0, 0, 1, 1, 0, 1, 1],
                  [0, 0, 0, 0, 1, 1, 1, 1, 1, 1, 1, 1], [1, 1, 1, 1, 0, 0, 0, 0, 0, 0, 0, 0],
                  [0, 0, 0, 0, 1, 1, 1, 1, 0, 0, 0, 0], [1, 1, 0, 0, 1, 1, 0, 0, 1, 1, 0, 0],
                  [1, 0, 1, 0, 1, 0, 1, 0, 1, 0, 1, 0], [0, 1, 0, 1, 0, 1, 0, 1, 0, 1, 0, 1],
                  [1, 0, 0, 1, 1, 0, 0, 1, 1, 0, 0, 1], [0, 1, 1, 0, 0, 1, 1, 0, 0, 1, 1, 0]], np.int64)
    rows = np.concatenate([a.T, np.eye(SYN, dtype=np.int64)], axis=1)
    masks = np.tile((rows * 2 ** np.arange(LAT)).sum(axis=1).astype(np.int32), (P, 1))
    number = np.arange(1, FR * E + 1)
    prefixes = np.zeros((NS, 3, FR * E), f4)
    prefixes[:, 0] = number[None, :] <= np.array(PREFIX)[:, None]
    prefixes[:, 1] = number
    prefixes[:, 2] = np.log(number)
    return con, prefixes, basis, masks


_INS = ["L0_attn_x", "L0_attn_W_el", "L0_attn_b_el", "L0_attn_W_le", "L0_attn_b_le",
        "L0_ffn_w1", "L0_ffn_b1", "L0_ffn_w2", "L0_ffn_b2"]


def kernel(**inputs):
    import numpy as np
    import concourse.bacc as bacc
    from concourse.bass_utils import run_bass_kernel_spmd as run

    nc = bacc.Bacc("TRN2", target_bir_lowering=False, num_devices=1)
    arrays, args = {}, []
    for name in _INS:
        arrays[name] = np.ascontiguousarray(inputs[name])
    for name, a in zip(("consts", "prefixes", "basis", "masks"), constants()):
        arrays[name] = a
    for name, a in arrays.items():
        args.append(nc.dram_tensor(name, a.shape, mybir.dt.from_np(a.dtype), kind="ExternalInput").ap())
    out = nc.dram_tensor("out", (2, 4096, E), F32, kind="ExternalOutput").ap()
    build(nc, *args, out)
    r = run(nc, [arrays], core_ids=[0])
    return r.results[0]["out"]
```

```python
import math
from contextlib import ExitStack

import concourse.bass as bass
from concourse import mybir

F32, F32R, BF16, I32 = mybir.dt.float32, mybir.dt.float32r, mybir.dt.bfloat16, mybir.dt.int32
ALU = mybir.AluOpType
ACT = mybir.ActivationFunctionType
AX = mybir.AxisListType

P = 128
TOKENS, E, HID, LAT, SYN = 2 * 4096, 256, 1024, 24, 12
TILES = TOKENS // P
CT = 4
CTOK = CT * P
CHUNKS = TILES // CT
KB = E // P
MB = HID // P
PAIRS = CT // 2
CE = E + LAT
HR = 4
BANK = 512
W1_PARTS = ((0, 2), (2, 4), (4, MB))
W2_PARTS = ((0, 4), (4, MB))
SCALES = (2, 4, 8, 16, 32)
NS = len(SCALES)
PREFIX = [s * s for s in SCALES]
FR = max(PREFIX) // E
LN_EPS = 1e-5
SEG = 32
IDLE = 12
HALF = CT // 2
HEAD = 1
LAST_PIECES = ((0, 2), (2, 3), (3, 4))
PRIMED = 1
ROWS_LE = LAT + 2

SINE = [(-1.0) ** n / math.factorial(2 * n + 1) for n in range(8)]

K_ID = 0
K_INVN = K_ID + P
K_COEF = K_INVN + 1
K_KA = K_COEF + P
K_KA2 = K_KA + KB
K_WK = K_KA2 + KB
K_POW2 = K_WK + 2 * KB
K_END = K_POW2 + LAT


def build(nc, x, w_el, b_el, w_le, b_le, w1, b1, w2, b2, consts, prefixes, basis, masks, out):
    ctx = ExitStack()
    with ctx:
        def sb(name, shape, dt):
            return ctx.enter_context(nc.sbuf_tensor(name, shape, dt))

        def ps(name, shape, dt):
            return ctx.enter_context(nc.psum_tensor(name, shape, dt))

        def sem(name):
            return ctx.enter_context(nc.semaphore(name))

        x_sb = sb("x_sb", [P, TILES * E], F32)
        xn = sb("xn", [P, CT, E], F32)
        xT_hi = [sb(f"xT_hi{i}", [P, KB, CTOK], F32R) for i in range(2)]
        xT_lo = [sb(f"xT_lo{i}", [P, KB, CTOK], F32R) for i in range(2)]
        h = [sb(f"h{i}", [P, CTOK], F32) for i in range(2)]
        h_hi = [sb(f"h_hi{i}", [P, CTOK], F32R) for i in range(HR)]
        h_lo = [sb(f"h_lo{i}", [P, CTOK], F32R) for i in range(HR)]
        w1_f = sb("w1_f", [P, KB, HID], F32)
        w1_hi = sb("w1_hi", [P, KB, HID], F32R)
        w1_lo = sb("w1_lo", [P, KB, HID], F32R)
        w2_f = sb("w2_f", [P, MB, E], F32)
        w2_hi = sb("w2_hi", [P, MB, E], F32R)
        w2_lo = sb("w2_lo", [P, MB, E], F32R)
        b1_sb = sb("b1_sb", [P, MB], F32)
        con = sb("con", [P, K_END], F32)
        mask_sb = sb("mask_sb", [P, SYN], I32)
        bel_sb = sb("bel_sb", [P, LAT], F32)
        wel_sb = sb("wel_sb", [P, KB, LAT], F32)
        basis_sb = sb("basis_sb", [P, KB, E], F32)
        basis_w = sb("basis_w", [P, KB, E], F32)
        c_f = sb("c_f", [P, E], F32)
        c_hi = sb("c_hi", [P, KB, CE], F32R)
        c_lo = sb("c_lo", [P, KB, CE], F32R)
        stats = sb("stats", [P, CT, 6], F32)
        mv = [sb(f"mv{i}", [P, CT, 2], F32) for i in range(2)]
        var_eps = sb("var_eps", [P, CT], F32)
        rstd = [sb(f"rstd{i}", [P, CT], F32) for i in range(2)]
        eps = sb("eps", [P, CT], F32)
        early = sb("early", [P, CT], F32)
        idle = sb("idle", [P, BANK], BF16)
        minus_half = sb("minus_half", [P, CT], F32)
        fr_x = sb("fr_x", [NS, FR, E], F32)
        fr_tab = sb("fr_tab", [NS, 3, FR * E], F32)
        fr_part = sb("fr_part", [NS, FR * E], F32)
        fr_sum = sb("fr_sum", [NS, 1], F32)
        fr_mean = sb("fr_mean", [NS, 1], F32)
        fr_cnt = sb("fr_cnt", [NS, 1], F32)
        fr_cnt1 = sb("fr_cnt1", [NS, 1], F32)
        fr_ln = sb("fr_ln", [NS, 1], F32)
        fr_d = sb("fr_d", [P, 8], F32)
        wave = sb("wave", [P, 4, 2 * KB], F32)
        bits = sb("bits", [P, 2, LAT], F32)
        weighed = sb("weighed", [P, 2, LAT], F32)
        word = sb("word", [P, 2, 1], I32)
        met = sb("met", [P, 2, SYN], I32)
        syn = sb("syn", [P, 2, SYN], F32)
        weight = sb("weight", [P, 2, 1], F32)
        flips = sb("flips", [P, 2, SYN], F32)
        cor = sb("cor", [P, 2, 3, SEG], BF16)
        cor_T = sb("cor_T", [3 * SEG, 2 * P], BF16)
        id_bf = sb("id_bf", [P, P], BF16)
        le_f = sb("le_f", [ROWS_LE, E], F32)
        le_r1 = sb("le_r1", [ROWS_LE, E], F32)
        le_mid = sb("le_mid", [ROWS_LE, E], BF16)
        le3 = sb("le3", [3 * SEG, E], BF16)

        p_h = ps("p_h", [P, 2, BANK], F32)
        p_o = ps("p_o", [P, CT, E], F32)
        p_c = ps("p_c", [P, 2, BANK], F32)
        p_t = ps("p_t", [P, BANK], F32)
        p_g = ps("p_g", [P, 2 * BANK], BF16)

        x_in = [sem("x_even"), sem("x_odd")]
        x_head = sem("x_head")
        w1_in = [sem(f"w1_in{i}") for i in range(len(W1_PARTS))]
        w2_in = [sem(f"w2_in{i}") for i in range(len(W2_PARTS))]
        b1_in, con_in, fr_in = sem("b1_in"), sem("con_in"), sem("fr_in")
        basis_in, small_in, le_in = sem("basis_in"), sem("small_in"), sem("le_in")
        stored = sem("stored")
        idle_set = sem("idle_set")
        pool_set = sem("pool_set")
        id_ready = sem("id_ready")
        w1_hi_ready, w1_ready = sem("w1_hi_ready"), sem("w1_ready")
        w2_hi_ready, w2_ready = sem("w2_hi_ready"), sem("w2_ready")
        logged = sem("logged")
        dim_made = sem("dim_made")
        basis_wd, c_made, c_copied = sem("basis_wd"), sem("c_made"), sem("c_copied")
        cw_made, c_hi_ready, c_ready = sem("cw_made"), sem("c_hi_ready"), sem("c_ready")
        le_ready = sem("le_ready")
        stat_done = sem("stat_done")
        veps_done, rstd_done = sem("veps_done"), sem("rstd_done")
        xn_done = sem("xn_done")
        t_done = sem("t_done")
        t_hi, t_lo = sem("t_hi"), sem("t_lo")
        up_done = sem("up_done")
        gelu_done, h_hi_done, h_lo_done = sem("gelu_done"), sem("h_hi_done"), sem("h_lo_done")
        down_done = sem("down_done")
        ffn_out = sem("ffn_out")
        wave_done = sem("wave_done")
        cor_done, cor_t, cor_sb = sem("cor_done"), sem("cor_t"), sem("cor_sb")
        le_done = sem("le_done")
        pair_out = sem("pair_out")
        wave_added = sem("wave_added")
        half_down = sem("half_down")
        tile_out = sem("tile_out")
        link = sem("link")

        x_rows = x.rearrange("b s e -> (b s) e").rearrange("(p t) e -> p (t e)", p=P)
        out_rows = out.rearrange("b s e -> (b s) e").rearrange("(p t) e -> p (t e)", p=P)
        CW = CT * E

        def half_tokens(xt, g):
            return xt[:, :, g * HALF * P:(g + 1) * HALF * P]

        def branch_pair(n):
            return CHUNKS - 2 + n // PAIRS, n % PAIRS

        def half_bank(g):
            return p_c[:, g, :].rearrange("p (k t) -> p k t", k=KB)

        block = ctx.enter_context(nc.Block())

        @block.sync
        def _(sp):
            for cols, arrived in ((slice(0, HALF * E), x_head), (slice(HALF * E, CW), x_in[0])):
                sp.dma_start(x_sb[:, cols], x_rows[:, cols]).then_inc(arrived, 16)
            def load_w1(n):
                cols = slice(W1_PARTS[n][0] * P, W1_PARTS[n][1] * P)
                sp.dma_start(w1_f[:, :, cols], w1[:, cols].rearrange("(k p) h -> p k h", p=P)).then_inc(w1_in[n], 16)

            def load_w2(n):
                m0, m1 = W2_PARTS[n]
                sp.dma_start(w2_f[:, m0:m1, :],
                             w2[m0 * P:m1 * P, :].rearrange("(m p) e -> p m e", p=P)).then_inc(w2_in[n], 16)

            sp.dma_start(con[:], consts).then_inc(con_in, 16)
            load_w1(0)
            load_w1(1)
            load_w2(0)
            with nc.allow_non_contiguous_dma(reason="4 KB once"):
                sp.dma_start(b1_sb[:], b1.rearrange("(m p) -> p m", p=P)).then_inc(b1_in, 16)
            load_w1(2)
            sp.dma_start(x_sb[:, CW:2 * CW], x_rows[:, CW:2 * CW]).then_inc(x_in[1], 16)
            load_w2(1)
            sp.dma_start(fr_tab[:, :, :], prefixes).then_inc(fr_in, 16)
            sp.wait_ge(xn_done, 2)
            for n in range(NS):
                sp.dma_start(fr_x[n:n + 1, :, :], xn[0:1, :, :]).then_inc(fr_in, 16)
            sp.dma_start(basis_sb[:, :, :], basis.rearrange("(k p) e -> p k e", p=P)).then_inc(basis_in, 16)
            sp.dma_start(wel_sb[:, :, :], w_el.rearrange("(k p) l -> p k l", p=P)).then_inc(small_in, 16)
            sp.dma_start(mask_sb[:], masks).then_inc(small_in, 16)
            sp.dma_start(bel_sb[:], b_el.partition_broadcast(P)).then_inc(small_in, 16)
            sp.dma_start(le_f[0:LAT, :], w_le).then_inc(le_in, 16)
            sp.dma_start(le_f[LAT:LAT + 1, :], b_le[None, :]).then_inc(le_in, 16)
            sp.dma_start(le_f[LAT + 1:LAT + 2, :], b2[None, :]).then_inc(le_in, 16)
            with sp.Fori(1, CHUNKS // 2) as i:
                for par in range(2):
                    sp.wait_ge(x_in[par], i * 16)
                    at = i * (2 * CW) + par * CW
                    sp.dma_start(x_sb[:, bass.ds(at, CW)], x_rows[:, bass.ds(at, CW)]).then_inc(x_in[par], 16)
            with sp.Fori(0, (CHUNKS - 1) * PAIRS) as n:
                sp.wait_ge(pair_out, PRIMED + n + 1)
                sp.dma_start(out_rows[:, bass.ds(n * (2 * E), 2 * E)],
                             x_sb[:, bass.ds(n * (2 * E), 2 * E)]).then_inc(stored, 16)
            for n, (j0, j1) in enumerate(LAST_PIECES):
                sp.wait_ge(tile_out, n + 1)
                cols = slice((TILES - CT + j0) * E, (TILES - CT + j1) * E)
                sp.dma_start(out_rows[:, cols], x_sb[:, cols]).then_inc(stored, 16)
            sp.wait_ge(stored, 16 * ((CHUNKS - 1) * PAIRS + len(LAST_PIECES)))

        @block.gpsimd
        def _(pool):
            nc.gpsimd.memset(eps[:], LN_EPS).then_inc(pool_set, 1)
            nc.gpsimd.memset(minus_half[:], -0.5).then_inc(pool_set, 1)
            pool.wait_ge(pool_set, 2)

            def inverse_root(step, par, tiles=slice(0, CT)):
                pool.wait_ge(stat_done, step + 1)
                nc.gpsimd.tensor_tensor(var_eps[:, tiles], mv[par][:, tiles, 1], eps[:, tiles],
                                        ALU.add).then_inc(veps_done, 1)
                pool.wait_ge(veps_done, step + 1)
                nc.gpsimd.tensor_tensor(rstd[par][:, tiles], var_eps[:, tiles], minus_half[:, tiles],
                                        ALU.pow).then_inc(rstd_done, 1)

            for g in range(2):
                inverse_root(g, 0, slice(g * HALF, (g + 1) * HALF))
            cols = slice(W1_PARTS[2][0] * P, W1_PARTS[2][1] * P)
            pool.wait_ge(w1_hi_ready, 3)
            pool.wait_ge(w1_ready, 2)
            nc.gpsimd.tensor_tensor(w1_lo[:, :, cols], w1_f[:, :, cols], w1_hi[:, :, cols].bitcast(F32),
                                    ALU.subtract).then_inc(w1_ready, 1)
            inverse_root(1 + HEAD, 1)
            m0, m1 = W2_PARTS[1]
            pool.wait_ge(w2_hi_ready, 2)
            pool.wait_ge(w2_ready, 1)
            nc.gpsimd.tensor_tensor(w2_lo[:, m0:m1, :], w2_f[:, m0:m1, :], w2_hi[:, m0:m1, :].bitcast(F32),
                                    ALU.subtract).then_inc(w2_ready, 1)
            with pool.Fori(0, (CHUNKS - 2) // 2) as i:
                for u in range(2):
                    inverse_root(2 * i + (2 + HEAD) + u, u)

        @block.scalar
        def _(act):
            act.sem_inc(cor_sb, PRIMED)
            act.wait_ge(pool_set, 2)
            nc.scalar.activation(early[:], eps[:], ACT.Gelu)

            def transposed_hi(c, par, k):
                act.wait_ge(t_done, KB * c + k + 1)
                nc.scalar.copy(xT_hi[par][:, k, :], p_t[:]).then_inc(t_hi, 1)

            def gelu(c, m, first=False):
                act.wait_ge(up_done, MB * c + m + 1)
                if not (first and m < 2):
                    act.wait_ge(h_lo_done, MB * c + m - 1)
                nc.scalar.activation(h[m % 2][:], p_h[:, m % 2, :], ACT.Gelu,
                                     bias=b1_sb[:, m:m + 1]).then_inc(gelu_done, 1)

            def hidden_hi(c, m, first=False):
                act.wait_ge(gelu_done, MB * c + m + 1)
                if not (first and m < HR):
                    act.wait_ge(down_done, MB * c + m + 1 - HR)
                nc.scalar.copy(h_hi[m % HR][:], h[m % 2][:]).then_inc(h_hi_done, 1)

            def corrected_copy(c, q):
                act.wait_ge(cor_t, PRIMED + PAIRS * c + q + 1)
                act.wait_ge(le_done, PRIMED + PAIRS * c + q)
                nc.scalar.copy(cor_T[:], p_g[0:3 * SEG, 0:2 * P]).then_inc(cor_sb, 1)

            def chunk(c, par):
                for m in range(MB):
                    gelu(c, m)
                    if m == MB - 1:
                        transposed_hi(c + 1, 1 - par, 1)
                    hidden_hi(c, m)
                    if m == 3:
                        corrected_copy(c - 1, 0)
                    if m == 6:
                        transposed_hi(c + 1, 1 - par, 0)
                corrected_copy(c - 1, 1)

            def last_chunk(c):
                for m in range(MB):
                    gelu(c, m)
                    if m >= 2 and m % 2 == 0:
                        corrected_copy(*branch_pair(m // 2 - 1))
                    hidden_hi(c, m)
                corrected_copy(*branch_pair(3))

            def w1_part_hi(n):
                cols = slice(W1_PARTS[n][0] * P, W1_PARTS[n][1] * P)
                act.wait_ge(w1_in[n], 16)
                nc.scalar.copy(w1_hi[:, :, cols], w1_f[:, :, cols]).then_inc(w1_hi_ready, 1)

            def w2_part_hi(n):
                m0, m1 = W2_PARTS[n]
                act.wait_ge(w2_in[n], 16)
                nc.scalar.copy(w2_hi[:, m0:m1, :], w2_f[:, m0:m1, :]).then_inc(w2_hi_ready, 1)

            w1_part_hi(0)
            act.wait_ge(con_in, 16)
            nc.scalar.copy(id_bf[:], con[:, K_ID:K_ID + P]).then_inc(id_ready, 1)
            for g in range(2):
                act.wait_ge(t_done, g + 1)
                nc.scalar.copy(half_tokens(xT_hi[0], g), half_bank(g)).then_inc(t_hi, 1)
            w1_part_hi(1)
            w2_part_hi(0)
            act.wait_ge(b1_in, 16)
            for m in range(MB):
                gelu(0, m, first=True)
                hidden_hi(0, m, first=True)
                if m == 0:
                    w1_part_hi(2)
                if m == 2:
                    w2_part_hi(1)
                if m >= 6:
                    transposed_hi(1, 1, m - 6)
            act.wait_ge(c_copied, 1)
            nc.scalar.copy(c_hi[:, 0, 0:E], c_f[:])
            nc.scalar.copy(c_hi[:, 1, 0:P], c_f[:, P:E])
            nc.scalar.copy(c_hi[:, 1, P:E], c_f[:, 0:P])
            act.wait_ge(cw_made, 1)
            nc.scalar.copy(c_hi[:, :, E:CE], p_c[:, :, E:CE]).then_inc(c_hi_ready, 1)

            with act.Fori(0, (CHUNKS - 2) // 2) as i:
                for u in range(2):
                    chunk(2 * i + 1 + u, 1 - u)
            last_chunk(CHUNKS - 1)

        @block.vector
        def _(dve):
            dve.sem_inc(pair_out, PRIMED)
            nc.vector.memset(idle[:], 0.0).then_inc(idle_set, 1)
            links = [0]

            def then(ins):
                links[0] += 1
                ins.then_inc(link, 1)
                dve.wait_ge(link, links[0])

            def statistics(c, par):
                dve.wait_ge(x_in[par], 8 * (c - par) + 16)
                for j in range(CT):
                    last = nc.vector.bn_stats(stats[:, j, :], x_chunk(c)[:, j, :])
                return last

            def x_chunk(c):
                return x_sb[:, bass.ds(c * CW, CW)].rearrange("p (j e) -> p j e", e=E)

            def aggregate(par, tiles=range(CT)):
                for j in tiles:
                    last = nc.vector.bn_aggr(mv[par][:, j, :], stats[:, j, :])
                last.then_inc(stat_done, 1)

            def normalise(c, par, g=None):
                if g is None:
                    dve.wait_ge(rstd_done, c + HEAD + 1)
                    dve.wait_ge(t_done, KB * c)
                    tiles = range(CT)
                else:
                    dve.wait_ge(rstd_done, g + 1)
                    tiles = range(g * HALF, (g + 1) * HALF)
                for j in tiles:
                    last = nc.vector.tensor_scalar(xn[:, j, :], x_chunk(c)[:, j, :], mv[par][:, j, 0:1],
                                                   rstd[par][:, j:j + 1], ALU.subtract, ALU.mult)
                last.then_inc(xn_done, 1)

            def transposed_lo(c, par, k):
                dve.wait_ge(t_hi, KB * c + k + 1)
                nc.vector.tensor_tensor(xT_lo[par][:, k, :], p_t[:], xT_hi[par][:, k, :].bitcast(F32),
                                        ALU.subtract).then_inc(t_lo, 1)

            def hidden_lo(c, m):
                dve.wait_ge(h_hi_done, MB * c + m + 1)
                nc.vector.tensor_tensor(h_lo[m % HR][:], h[m % 2][:], h_hi[m % HR][:].bitcast(F32),
                                        ALU.subtract).then_inc(h_lo_done, 1)

            def add_ffn(c):
                dve.wait_ge(down_done, MB * (c + 1))
                for q in range(PAIRS):
                    seg = x_chunk(c)[:, 2 * q:2 * q + 2, :]
                    nc.vector.tensor_tensor(seg, p_o[:, 2 * q:2 * q + 2, :], seg, ALU.add).then_inc(ffn_out, 1)

            def correct(c, q, hops, between=None):
                dve.wait_ge(wave_done, PAIRS * c + q + 1)
                lat = p_c[:, :, E:CE]
                bel = bel_sb[:, :].unsqueeze(1).broadcast_to([P, 2, LAT])
                pow2 = con[:, K_POW2:K_POW2 + LAT].unsqueeze(1).broadcast_to([P, 2, LAT])
                mask = mask_sb[:, :].unsqueeze(1).broadcast_to([P, 2, SYN])
                hops(nc.vector.scalar_tensor_tensor(out=bits[:], in0=lat, scalar=-1.0, in1=bel,
                                                    op0=ALU.mult, op1=ALU.is_lt))
                hops(nc.vector.tensor_tensor(weighed[:], bits[:], pow2, ALU.mult))
                with nc.allow_low_precision(reason="distinct powers of two under 2^24: an exact sum"):
                    summed = nc.vector.tensor_reduce(word[:], weighed[:], AX.X, ALU.add)
                if between:
                    between()
                hops(summed)
                hops(nc.vector.tensor_tensor(met[:], word[:].broadcast_to([P, 2, SYN]), mask, ALU.bitwise_and))
                hops(nc.vector.tensor_scalar(syn[:], met[:], 0.0, None, ALU.is_gt))
                hops(nc.vector.tensor_reduce(weight[:], syn[:], AX.X, ALU.add))
                hops(nc.vector.scalar_tensor_tensor(out=flips[:], in0=weight[:].broadcast_to([P, 2, SYN]),
                                                    scalar=3.0, in1=syn[:], op0=ALU.is_le, op1=ALU.mult))
                dve.wait_ge(cor_t, PRIMED + PAIRS * c + q)
                thrice = [P, 2, 3, SYN]
                nc.vector.tensor_tensor(cor[:, :, :, 0:SYN], bits[:, :, 0:SYN].unsqueeze(2).broadcast_to(thrice),
                                        flips[:].unsqueeze(2).broadcast_to(thrice), ALU.not_equal)
                nc.vector.tensor_copy(cor[:, :, :, SYN:LAT],
                                      bits[:, :, SYN:LAT].unsqueeze(2).broadcast_to(thrice)).then_inc(cor_done, 1)

            def add_wave(c, q, last=False):
                dve.wait_ge(le_done, PRIMED + PAIRS * c + q + 1)
                if not last:
                    dve.wait_ge(ffn_out, PAIRS * (c + 1))
                seg = x_chunk(c)[:, 2 * q:2 * q + 2, :]
                nc.vector.tensor_tensor(seg, p_c[:, :, 0:E], seg, ALU.add).then_inc(wave_added if last else pair_out, 1)

            def chunk(c, par, hops):
                add_ffn(c - 1)
                hidden_lo(c, 0)
                hops(statistics(c + 1, 1 - par))
                hidden_lo(c, 1)
                aggregate(1 - par)
                correct(c - 1, 0, hops)
                hidden_lo(c, 2)
                hidden_lo(c, 3)
                normalise(c + 1, 1 - par)
                add_wave(c - 1, 0)
                hidden_lo(c, 4)
                hidden_lo(c, 5)
                correct(c - 1, 1, hops)
                hidden_lo(c, 6)
                transposed_lo(c + 1, 1 - par, 0)
                transposed_lo(c + 1, 1 - par, 1)
                hidden_lo(c, 7)
                add_wave(c - 1, 1)

            def last_chunk(c, hops):
                add_ffn(c - 1)
                for n in range(2 * PAIRS):
                    correct(*branch_pair(n), hops, between=lambda: hidden_lo(c, 2 * n + (n > 0)))
                    if n == 0:
                        hidden_lo(c, 1)
                    if n < 2 * PAIRS - 1:
                        hidden_lo(c, 2 * n + 2)
                        add_wave(*branch_pair(n), last=n >= PAIRS)
                pieces = [x_chunk(c)[:, j0:j1, :] for j0, j1 in LAST_PIECES]
                for n, (piece, (j0, j1)) in enumerate(zip(pieces, LAST_PIECES)):
                    if n == 1:
                        add_wave(c, PAIRS - 1, last=True)
                        dve.wait_ge(wave_added, PAIRS)
                    dve.wait_ge(*((half_down, 1) if n == 0 else (down_done, MB * (c + 1))))
                    nc.vector.tensor_tensor(piece, p_o[:, j0:j1, :], piece, ALU.add).then_inc(tile_out, 1)

            def w1_part_lo(n):
                cols = slice(W1_PARTS[n][0] * P, W1_PARTS[n][1] * P)
                dve.wait_ge(w1_hi_ready, n + 1)
                nc.vector.tensor_tensor(w1_lo[:, :, cols], w1_f[:, :, cols], w1_hi[:, :, cols].bitcast(F32),
                                        ALU.subtract).then_inc(w1_ready, 1)

            def w2_part_lo(n):
                m0, m1 = W2_PARTS[n]
                dve.wait_ge(w2_hi_ready, n + 1)
                nc.vector.tensor_tensor(w2_lo[:, m0:m1, :], w2_f[:, m0:m1, :], w2_hi[:, m0:m1, :].bitcast(F32),
                                        ALU.subtract).then_inc(w2_ready, 1)

            halves = [range(g * HALF, (g + 1) * HALF) for g in range(2)]
            for g, arrived in enumerate((x_head, x_in[0])):
                dve.wait_ge(arrived, 16)
                for j in halves[g]:
                    last = nc.vector.bn_stats(stats[:, j, :], x_chunk(0)[:, j, :])
                then(last)
                aggregate(0, halves[g])
            normalise(0, 0, 0)
            normalise(0, 0, 1)
            w1_part_lo(0)
            for g in range(2):
                dve.wait_ge(t_hi, g + 1)
                nc.vector.tensor_tensor(half_tokens(xT_lo[0], g), half_bank(g), half_tokens(xT_hi[0], g).bitcast(F32),
                                        ALU.subtract).then_inc(t_lo, 1)
            w1_part_lo(1)
            w2_part_lo(0)
            hidden_lo(0, 0)
            then(statistics(1, 1))
            aggregate(1)
            hidden_lo(0, 1)
            hidden_lo(0, 2)
            dve.wait_ge(fr_in, 16 * (NS + 1))
            fr_flat = fr_x[:, :, :].rearrange("p a e -> p (a e)")
            then(nc.vector.scalar_tensor_tensor(out=fr_part[:], in0=fr_flat, scalar=1.0, in1=fr_tab[:, 0, :],
                                                op0=ALU.mult, op1=ALU.mult, accum_out=fr_sum[:]))
            then(nc.vector.tensor_scalar(fr_mean[:], fr_sum[:], con[0:NS, K_INVN:K_INVN + 1], None, ALU.mult))
            hidden_lo(0, 3)
            then(nc.vector.scalar_tensor_tensor(out=fr_part[:], in0=fr_flat, scalar=fr_mean[:, 0:1],
                                                in1=fr_tab[:, 0, :], op0=ALU.is_gt, op1=ALU.mult,
                                                accum_out=fr_cnt[:]))
            then(nc.vector.tensor_scalar(fr_cnt1[:], fr_cnt[:], 1.0, None, ALU.max))
            hidden_lo(0, 4)
            nc.vector.scalar_tensor_tensor(out=fr_part[:], in0=fr_tab[:, 1, :], scalar=fr_cnt1[:, 0:1],
                                           in1=fr_tab[:, 2, :], op0=ALU.is_equal, op1=ALU.mult,
                                           accum_out=fr_ln[:]).then_inc(logged, 1)
            normalise(1, 1)
            hidden_lo(0, 5)
            dve.wait_ge(dim_made, 1)
            then(nc.vector.tensor_scalar(fr_d[:, 1:2], p_c[:, 0, 0:1], 1.0, 2.0, ALU.max, ALU.min))
            D, om, od, a, b = (fr_d[:, k:k + 1] for k in (1, 2, 3, 4, 5))
            then(nc.vector.tensor_scalar(om, D, 0.2, 1.0, ALU.mult, ALU.add))
            nc.vector.tensor_scalar(a, D, 0.5, 1.0, ALU.mult, ALU.add)
            nc.vector.tensor_scalar(b, D, 0.1, None, ALU.mult)
            then(nc.vector.tensor_tensor(od, D, om, ALU.mult))
            ka, ka2 = con[:, K_KA:K_KA + KB], con[:, K_KA2:K_KA2 + KB]
            nc.vector.tensor_scalar(wave[:, 0, 0:KB], ka, a, od, ALU.mult, ALU.add)
            then(nc.vector.tensor_scalar(wave[:, 0, KB:2 * KB], ka2, b, od, ALU.mult, ALU.add))
            then(nc.vector.tensor_tensor(wave[:, 1, KB:2 * KB], wave[:, 0, KB:2 * KB], ka, ALU.subtract))
            then(nc.vector.tensor_scalar(wave[:, 2, 0:KB], wave[:, 0, 0:KB], -1.0, math.pi, ALU.mult, ALU.add))
            then(nc.vector.tensor_scalar(wave[:, 2, KB:2 * KB], wave[:, 1, KB:2 * KB], -1.0, math.pi / 2,
                                         ALU.mult, ALU.add))
            t, s, weighted, series = (wave[:, k, :] for k in (2, 0, 1, 3))
            nc.vector.tensor_tensor(weighted, t, con[:, K_WK:K_WK + 2 * KB], ALU.mult)
            then(nc.vector.tensor_tensor(s, t, t, ALU.mult))
            then(nc.vector.tensor_scalar(series, s, SINE[-1], None, ALU.mult))
            for n, c in enumerate(reversed(SINE[1:-1])):
                then(nc.vector.scalar_tensor_tensor(out=series, in0=series, scalar=c, in1=s,
                                                    op0=ALU.add, op1=ALU.mult))
                if n == 1:
                    hidden_lo(0, 6)
                    transposed_lo(1, 1, 0)
            then(nc.vector.scalar_tensor_tensor(out=series, in0=series, scalar=SINE[0], in1=weighted,
                                                op0=ALU.add, op1=ALU.mult))
            dve.wait_ge(basis_in, 16)
            for k in range(KB):
                nc.vector.tensor_scalar(basis_w[:, k, :], basis_sb[:, k, :], series[:, k:k + 1],
                                        series[:, KB + k:KB + k + 1], ALU.mult, ALU.mult).then_inc(basis_wd, 1)
            hidden_lo(0, 7)
            dve.wait_ge(c_made, 1)
            nc.vector.tensor_copy(c_f[:], p_c[:, 0, 0:E]).then_inc(c_copied, 1)
            transposed_lo(1, 1, 1)
            then(nc.vector.memset(le3[:], 0.0))
            then(nc.vector.memset(cor[:], 0.0))
            nc.vector.memset(cor[:, :, :, LAT:LAT + 2], 1.0)
            dve.wait_ge(le_in, 48)
            then(nc.vector.tensor_copy(le3[0:ROWS_LE, :], le_f[:]))
            then(nc.vector.tensor_tensor(le_r1[:], le_f[:], le3[0:ROWS_LE, :], ALU.subtract))
            then(nc.vector.tensor_copy(le_mid[:], le_r1[:]))
            nc.vector.tensor_copy(le3[SEG:SEG + ROWS_LE, :], le_mid[:])
            nc.vector.tensor_tensor(le3[2 * SEG:2 * SEG + ROWS_LE, :], le_r1[:], le_mid[:],
                                    ALU.subtract).then_inc(le_ready, 1)
            dve.wait_ge(small_in, 48)
            dve.wait_ge(c_hi_ready, 1)
            nc.vector.tensor_tensor(c_lo[:, 0, 0:E], c_f[:], c_hi[:, 0, 0:E].bitcast(F32), ALU.subtract)
            nc.vector.tensor_tensor(c_lo[:, 1, 0:P], c_f[:, P:E], c_hi[:, 1, 0:P].bitcast(F32), ALU.subtract)
            nc.vector.tensor_tensor(c_lo[:, 1, P:E], c_f[:, 0:P], c_hi[:, 1, P:E].bitcast(F32), ALU.subtract)
            nc.vector.tensor_tensor(c_lo[:, :, E:CE], p_c[:, :, E:CE], c_hi[:, :, E:CE].bitcast(F32),
                                    ALU.subtract).then_inc(c_ready, 1)

            base = links[0]
            per_chunk = 1 + 7 * PAIRS

            def hopper(start):
                n = [0]

                def hop(ins):
                    n[0] += 1
                    ins.then_inc(link, 1)
                    dve.wait_ge(link, start + n[0])
                return hop

            with dve.Fori(0, (CHUNKS - 2) // 2) as i:
                for u in range(2):
                    chunk(2 * i + 1 + u, 1 - u, hopper(i * (2 * per_chunk) + (base + u * per_chunk)))
            tail = hopper(base + (CHUNKS - 2) * per_chunk)
            last_chunk(CHUNKS - 1, tail)

        @block.tensor
        def _(pe):
            pe.sem_inc(le_done, PRIMED)
            pe.sem_inc(cor_t, PRIMED)
            mm = nc.tensor.matmul

            def transpose_block(c, k):
                if k == 0:
                    pe.wait_ge(xn_done, c + HEAD + 1)
                pe.wait_ge(t_lo, KB * c + k)
                for j in range(CT):
                    last = nc.tensor.transpose(p_t[:, j * P:(j + 1) * P], xn[:, j, k * P:(k + 1) * P],
                                               con[:, K_ID:K_ID + P])
                last.then_inc(t_done, 1)

            def up(c, par, m, first=False):
                if m == 0 and not first:
                    pe.wait_ge(t_lo, KB * (c + 1))
                for n, (m0, _) in enumerate(W1_PARTS):
                    if first and m == m0:
                        pe.wait_ge(*((w1_hi_ready, 1) if n == 0 else (w1_ready, n + 1)))
                if not (first and m < 2):
                    pe.wait_ge(gelu_done, MB * c + m - 1)
                groups = 2 if first and m == 0 else 1
                for g in range(groups):
                    tok = slice(g * CTOK // groups, (g + 1) * CTOK // groups)
                    n = 0
                    for w, xt in ((w1_hi, xT_hi), (w1_lo, xT_hi), (w1_hi, xT_lo)):
                        if groups == 2 and w is w1_hi:
                            pe.wait_ge(t_hi if xt is xT_hi else t_lo, g + 1)
                        if first and m == W1_PARTS[0][0] and w is w1_lo:
                            pe.wait_ge(w1_ready, 1)
                        for k in range(KB):
                            last = mm(p_h[:, m % 2, tok], w[:, k, m * P:(m + 1) * P], xt[par][:, k, tok],
                                      start=(n == 0), stop=(n == 3 * KB - 1))
                            n += 1
                last.then_inc(up_done, 1)

            def down(c, m, first=False, tiles=range(CT), done=down_done):
                pe.wait_ge(h_lo_done, MB * c + m + 1)
                if m == 0 and not first:
                    pe.wait_ge(ffn_out, PAIRS * c)
                for n, (m0, _) in enumerate(W2_PARTS):
                    if first and m == m0:
                        pe.wait_ge(w2_ready, n + 1)
                r = m % HR
                for j in tiles:
                    tok = slice(j * P, (j + 1) * P)
                    for n, (hp, w) in enumerate(((h_hi, w2_hi), (h_hi, w2_lo), (h_lo, w2_hi))):
                        last = mm(p_o[:, j, :], hp[r][:, tok], w[:, m, :], start=(m == 0 and n == 0 and j % 2 == 0),
                                  stop=(m == MB - 1 and n == 2), skip_group_check=True)
                last.then_inc(done, 1)

            def wave_products(c, par, q, free=None):
                pe.wait_ge(*(free or (pair_out, PRIMED + PAIRS * c + q)))
                pe.wait_ge(c_ready, 1)
                for r in range(2):
                    tok = slice((2 * q + r) * P, (2 * q + r + 1) * P)
                    n = 0
                    for k in range(KB):
                        for xt, cc in ((xT_hi, c_hi), (xT_hi, c_lo), (xT_lo, c_hi)):
                            last = mm(p_c[:, r, 0:CE], xt[par][:, k, tok], cc[:, k, :], start=(n == 0), stop=False,
                                      skip_group_check=True)
                            n += 1
                last.then_inc(wave_done, 1)

            def transpose_corrected(c, q):
                pe.wait_ge(cor_done, PAIRS * c + q + 1)
                pe.wait_ge(cor_sb, PRIMED + PAIRS * c + q)
                for r in range(2):
                    last = nc.tensor.transpose(p_g[0:3 * SEG, r * P:(r + 1) * P],
                                               cor[:, r, :, :].rearrange("p a s -> p (a s)"), id_bf[:])
                last.then_inc(cor_t, 1)

            def le_products(c, q):
                pe.wait_ge(cor_sb, PRIMED + PAIRS * c + q + 1)
                pe.wait_ge(le_ready, 1)
                for r in range(2):
                    last = mm(p_c[:, r, 0:E], cor_T[:, r * P:(r + 1) * P], le3[:], start=False, stop=True,
                              skip_group_check=True)
                last.then_inc(le_done, 1)

            def chunk(c, par):
                for m in range(MB):
                    up(c, par, m)
                    if m == 1:
                        wave_products(c - 1, 1 - par, 0)
                    if m == 4:
                        le_products(c - 1, 0)
                    if m == 5:
                        wave_products(c - 1, 1 - par, 1)
                    if m >= 6:
                        transpose_block(c + 1, m - 6)
                    if m == 7:
                        transpose_corrected(c - 1, 1)
                    if m >= 2:
                        down(c, m - 2)
                    if m == 3:
                        transpose_corrected(c - 1, 0)
                down(c, MB - 2)
                le_products(c - 1, 1)
                down(c, MB - 1)

            def last_chunk(c, par):
                def branch_products(n):
                    cc, q = branch_pair(n)
                    wave_products(cc, par if cc == c else 1 - par, q,
                                  free=(wave_added, n - PAIRS) if n > PAIRS else None)

                for m in range(MB):
                    up(c, par, m)
                    if m == 0:
                        branch_products(0)
                    if m >= 3 and m % 2 == 1:
                        branch_products(m // 2)
                    if m >= 2 and m % 2 == 0:
                        transpose_corrected(*branch_pair(m // 2 - 1))
                    if m >= 2:
                        down(c, m - 2)
                    if m >= 2 and m % 2 == 0:
                        le_products(*branch_pair(m // 2 - 1))
                down(c, MB - 2)
                transpose_corrected(*branch_pair(3))
                down(c, MB - 1, tiles=range(2), done=half_down)
                le_products(*branch_pair(3))
                down(c, MB - 1, tiles=range(2, CT))

            def circulant():
                pe.wait_ge(basis_wd, KB)
                for k in range(KB):
                    last = mm(p_c[:, 0, 0:E], basis_sb[:, k, 0:P], basis_w[:, k, :], start=(k == 0), stop=(k == KB - 1))
                last.then_inc(c_made, 1)

            def latent_products():
                pe.wait_ge(c_copied, 1)
                pe.wait_ge(small_in, 48)
                for i in range(KB):
                    for k in range(KB):
                        ab = c_f[:, P:E] if i != k else c_f[:, 0:P]
                        last = mm(p_c[:, i, E:CE], ab, wel_sb[:, k, :], start=(k == 0), stop=(k == KB - 1))
                last.then_inc(cw_made, 1)

            pe.wait_ge(idle_set, 1)
            for _ in range(IDLE):
                mm(p_o[:, 0:2, :], idle[:, 0:P], idle[:], start=True, stop=True)
            pe.wait_ge(con_in, 16)
            for g in range(2):
                pe.wait_ge(xn_done, g + 1)
                for k in range(KB):
                    for j in range(HALF):
                        last = nc.tensor.transpose(half_bank(g)[:, k, j * P:(j + 1) * P],
                                                   xn[:, g * HALF + j, k * P:(k + 1) * P], con[:, K_ID:K_ID + P])
                last.then_inc(t_done, 1)
            for m in range(MB):
                up(0, 0, m, first=True)
                if m == 6:
                    pe.wait_ge(logged, 1)
                    mm(p_c[:, 0, 0:1], con[0:NS, K_COEF:K_COEF + P], fr_ln[:], start=True, stop=True).then_inc(dim_made, 1)
                if m >= 2:
                    down(0, m - 2, first=True)
                if m == 6:
                    transpose_block(1, 0)
            down(0, MB - 2)
            transpose_block(1, 1)
            circulant()
            down(0, MB - 1)
            latent_products()
            pe.wait_ge(id_ready, 1)

            with pe.Fori(0, (CHUNKS - 2) // 2) as i:
                for u in range(2):
                    chunk(2 * i + 1 + u, 1 - u)
            last_chunk(CHUNKS - 1, 1)


def constants():
    import numpy as np

    f4 = np.float32
    con = np.zeros((P, K_END), f4)
    con[:, K_ID:K_ID + P] = np.eye(P, dtype=f4)
    con[0:NS, K_INVN] = [1.0 / n for n in PREFIX]
    lx = np.log(np.array(SCALES, np.float64))
    n = len(SCALES)
    den = n * np.sum(lx * lx) - np.sum(lx) ** 2
    con[0:NS, K_COEF:K_COEF + P] = (-(n * lx - np.sum(lx)) / den)[:, None]
    r = np.arange(E)
    freq = np.where(r <= E // 2, r, r - E // 2)
    ang = 2.0 * np.pi * ((freq[:, None] * r[None, :]) % E) / E
    basis = np.where((r <= E // 2)[:, None], np.cos(ang), np.sin(ang)).astype(f4)
    ka = (freq / E).astype(f4) + f4(1e-8)
    weight = np.where((r == 0) | (r == E // 2), 1.0, 2.0) / E
    by_block = lambda v: v.reshape(KB, P).T
    con[:, K_KA:K_KA + KB] = by_block(ka)
    con[:, K_KA2:K_KA2 + KB] = by_block(ka * ka)
    con[:, K_WK:K_WK + KB] = by_block(weight)
    con[:, K_WK + KB:K_WK + 2 * KB] = 1.0
    con[:, K_POW2:K_POW2 + LAT] = 2.0 ** np.arange(LAT)
    a = np.array([[1, 1, 1, 0, 1, 1, 1, 0, 0, 0, 1, 1], [1, 1, 0, 1, 1, 1, 0, 0, 0, 1, 1, 0],
                  [1, 0, 1, 1, 1, 0, 0, 0, 1, 1, 0, 1], [0, 1, 1, 1, 0, 0, 0, 1, 1, 0, 1, 1],
                  [0, 0, 0, 0, 1, 1, 1, 1, 1, 1, 1, 1], [1, 1, 1, 1, 0, 0, 0, 0, 0, 0, 0, 0],
                  [0, 0, 0, 0, 1, 1, 1, 1, 0, 0, 0, 0], [1, 1, 0, 0, 1, 1, 0, 0, 1, 1, 0, 0],
                  [1, 0, 1, 0, 1, 0, 1, 0, 1, 0, 1, 0], [0, 1, 0, 1, 0, 1, 0, 1, 0, 1, 0, 1],
                  [1, 0, 0, 1, 1, 0, 0, 1, 1, 0, 0, 1], [0, 1, 1, 0, 0, 1, 1, 0, 0, 1, 1, 0]], np.int64)
    rows = np.concatenate([a.T, np.eye(SYN, dtype=np.int64)], axis=1)
    masks = np.tile((rows * 2 ** np.arange(LAT)).sum(axis=1).astype(np.int32), (P, 1))
    number = np.arange(1, FR * E + 1)
    prefixes = np.zeros((NS, 3, FR * E), f4)
    prefixes[:, 0] = number[None, :] <= np.array(PREFIX)[:, None]
    prefixes[:, 1] = number
    prefixes[:, 2] = np.log(number)
    return con, prefixes, basis, masks


_INS = ["L0_attn_x", "L0_attn_W_el", "L0_attn_b_el", "L0_attn_W_le", "L0_attn_b_le",
        "L0_ffn_w1", "L0_ffn_b1", "L0_ffn_w2", "L0_ffn_b2"]


def kernel(**inputs):
    import numpy as np
    import concourse.bacc as bacc
    from concourse.bass_utils import run_bass_kernel_spmd as run

    nc = bacc.Bacc("TRN2", target_bir_lowering=False, num_devices=1)
    arrays, args = {}, []
    for name in _INS:
        arrays[name] = np.ascontiguousarray(inputs[name])
    for name, a in zip(("consts", "prefixes", "basis", "masks"), constants()):
        arrays[name] = a
    for name, a in arrays.items():
        args.append(nc.dram_tensor(name, a.shape, mybir.dt.from_np(a.dtype), kind="ExternalInput").ap())
    out = nc.dram_tensor("out", (2, 4096, E), F32, kind="ExternalOutput").ap()
    build(nc, *args, out)
    r = run(nc, [arrays], core_ids=[0])
    return r.results[0]["out"]
```
